# Optimizing a Trainium2 kernel written in Bass

```python
import numpy as np
import jax
import jax.numpy as jnp

def _softmax(x, axis=-1):
    return jax.nn.softmax(x, axis=axis)

def _gelu(x):
    return jax.nn.gelu(x, approximate=True)

def _silu(x):
    return jax.nn.silu(x)

def _sigmoid(x):
    return jax.nn.sigmoid(x)

def _layernorm(x, axis=-1, eps=1e-05):
    m = jnp.mean(x, axis=axis, keepdims=True)
    v = jnp.var(x, axis=axis, keepdims=True)
    return (x - m) / jnp.sqrt(v + eps)

def _scatter_add(tgt, idx, src, axis=0):
    return tgt.at[idx].add(src)

def _segment_sum(src, seg, n):
    return jax.ops.segment_sum(src, seg, n)
kernel_name = 'mk_prb_d2_jaxref_r8_bc46dc'

def setup_inputs(seed: int=0):
    np.random.seed(seed)
    _w = jnp.asarray

    def _L0_attn_setup():
        import jax, jax.numpy as jnp
        import numpy as np
        B, S, D = (1, 512, 128)
        H, W = (16, 64)
        HD = D // H
        key = jax.random.key(seed)
        k1, k2, k3 = jax.random.split(key, 3)
        x = jax.random.normal(k1, (B, S, D), dtype=jnp.float32)
        w_qkv = jax.random.normal(k2, (D, 3 * D), dtype=jnp.float32) * 0.02
        w_out = jax.random.normal(k3, (D, D), dtype=jnp.float32) * 0.02
        return {'x': x, 'w_qkv': w_qkv, 'w_out': w_out}
    _L0_attn_in = _L0_attn_setup()

    def _L0_ffn_setup():
        import jax, jax.numpy as jnp
        import numpy as np
        FP8_MAX = 448.0
        key = jax.random.key(seed)
        k_x, k_w, k_b = jax.random.split(key, 3)
        B, S, IN, OUT = (4, 1024, 128, 128)
        x = jax.random.normal(k_x, (B, S, IN), dtype=jnp.float32)
        w_fp32 = jax.random.normal(k_w, (OUT, IN), dtype=jnp.float32)
        weight_fp8 = w_fp32.astype(jnp.float8_e4m3fn).astype(jnp.float32)
        bias = jax.random.normal(k_b, (OUT,), dtype=jnp.float32)
        input_scale = jnp.ones((1,), dtype=jnp.float32)
        weight_scale = jnp.ones((1,), dtype=jnp.float32)
        return {'x': x, 'weight_fp8': weight_fp8, 'bias': bias, 'input_scale': input_scale, 'weight_scale': weight_scale}
    _L0_ffn_in = _L0_ffn_setup()

    def _L1_attn_setup():
        import jax, jax.numpy as jnp
        import numpy as np
        B, T, D = (2, 256, 128)
        HEAD_DIM, N_HEADS, N_HH, HEAD_V_DIM, CONV_SIZE = (128, 8, 3, 128, 4)

        def _short_conv(x, w):
            cs = w.shape[-1]
            t = x.shape[1]
            xp = jnp.pad(x, ((0, 0), (cs - 1, 0), (0, 0)))
            y = sum((xp[:, i:i + t, :] * w[:, i] for i in range(cs)))
            return jax.nn.silu(y)

        def _l2norm(x, eps=1e-06):
            return x * jax.lax.rsqrt(jnp.sum(x * x, -1, keepdims=True) + eps)

        def _forward(x, Wq, Wk, Wv, Wb, Wa, A_log, dt_bias, conv_q, conv_k, conv_v, Wg, rms_weight, Wo):
            b, t, _ = x.shape
            h, d, dv, nh = (N_HEADS, HEAD_DIM, HEAD_V_DIM, N_HH)
            q = _short_conv(x @ Wq, conv_q).reshape(b, t, h, d)
            k = _short_conv(x @ Wk, conv_k).reshape(b, t, nh, h, d).transpose(0, 1, 3, 2, 4)
            v = _short_conv(x @ Wv, conv_v).reshape(b, t, nh, h, dv).transpose(0, 1, 3, 2, 4)
            beta = 2.0 * jax.nn.sigmoid(x @ Wb).reshape(b, t, nh, h).transpose(0, 1, 3, 2)
            g = -jnp.exp(A_log) * jax.nn.softplus(x @ Wa + dt_bias)
            q = _l2norm(q) * d ** (-0.5)
            k = _l2norm(k)

            def step(S, inp):
                qt, kt, vt, bt, gt = inp
                S = S * jnp.exp(gt)[..., None, None]
                for i in range(nh):
                    ki, vi, bi = (kt[:, :, i], vt[:, :, i], bt[:, :, i])
                    kS = jnp.einsum('bhd,bhde->bhe', ki, S)
                    S = S + bi[..., None, None] * (ki[..., None] * (vi - kS)[:, :, None, :])
                o = jnp.einsum('bhd,bhde->bhe', qt, S)
                return (S, o)
            xs = tuple((jnp.moveaxis(a, 1, 0) for a in (q, k, v, beta, g)))
            S0 = jnp.zeros((b, h, d, dv), x.dtype)
            _, o = jax.lax.scan(step, S0, xs)
            o = jnp.moveaxis(o, 0, 1)
            gate = (x @ Wg).reshape(b, t, h, dv)
            o = o * jax.lax.rsqrt(jnp.mean(o * o, -1, keepdims=True) + 1e-05) * rms_weight
            o = o * jax.nn.silu(gate)
            return o.reshape(b, t, h * dv) @ Wo
        key = jax.random.key(seed)
        ks = jax.random.split(key, 16)
        h, d, dv, nh, cs = (N_HEADS, HEAD_DIM, HEAD_V_DIM, N_HH, CONV_SIZE)
        f = lambda k, shape, s=0.02: jax.random.normal(k, shape, jnp.float32) * s
        return {'x': f(ks[0], (B, T, D), 1.0), 'cos': f(ks[1], (T, d), 1.0), 'sin': f(ks[2], (T, d), 1.0), 'Wq': f(ks[3], (D, h * d)), 'Wk': f(ks[4], (D, h * d * nh)), 'Wv': f(ks[5], (D, h * dv * nh)), 'Wb': f(ks[6], (D, h * nh)), 'Wa': f(ks[7], (D, h)), 'A_log': jnp.log(jax.random.uniform(ks[8], (h,), jnp.float32, 0.5, 8.0)), 'dt_bias': f(ks[9], (h,), 0.1), 'conv_q': f(ks[10], (h * d, cs), 0.5), 'conv_k': f(ks[11], (h * d * nh, cs), 0.5), 'conv_v': f(ks[12], (h * dv * nh, cs), 0.5), 'Wg': f(ks[13], (D, h * dv)), 'rms_weight': jnp.ones((dv,), jnp.float32), 'Wo': f(ks[14], (h * dv, D))}
    _L1_attn_in = _L1_attn_setup()

    def _L1_ffn_setup():
        import jax, jax.numpy as jnp
        import numpy as np
        TOP_K = 2
        key = jax.random.key(seed)
        ks = jax.random.split(key, 6)
        B, T, H, E, F = (2, 256, 128, 8, 512)
        s = 0.02
        return {'hidden_states': jax.random.normal(ks[0], (B, T, H), dtype=jnp.float32), 'router_w': jax.random.normal(ks[1], (E, H), dtype=jnp.float32) * s, 'w1': jax.random.normal(ks[2], (E, F, H), dtype=jnp.float32) * s, 'b1': jax.random.normal(ks[3], (E, F), dtype=jnp.float32) * s, 'w2': jax.random.normal(ks[4], (E, H, F), dtype=jnp.float32) * s, 'b2': jax.random.normal(ks[5], (E, H), dtype=jnp.float32) * s}
    _L1_ffn_in = _L1_ffn_setup()
    _d = {'L0_attn_x': _L0_attn_in['x'], 'L0_attn_w_qkv': _L0_attn_in['w_qkv'], 'L0_attn_w_out': _L0_attn_in['w_out'], 'L0_ffn_weight_fp8': _L0_ffn_in['weight_fp8'], 'L0_ffn_bias': _L0_ffn_in['bias'], 'L0_ffn_input_scale': _L0_ffn_in['input_scale'], 'L0_ffn_weight_scale': _L0_ffn_in['weight_scale'], 'L1_attn_cos': _L1_attn_in['cos'], 'L1_attn_sin': _L1_attn_in['sin'], 'L1_attn_Wq': _L1_attn_in['Wq'], 'L1_attn_Wk': _L1_attn_in['Wk'], 'L1_attn_Wv': _L1_attn_in['Wv'], 'L1_attn_Wb': _L1_attn_in['Wb'], 'L1_attn_Wa': _L1_attn_in['Wa'], 'L1_attn_A_log': _L1_attn_in['A_log'], 'L1_attn_dt_bias': _L1_attn_in['dt_bias'], 'L1_attn_conv_q': _L1_attn_in['conv_q'], 'L1_attn_conv_k': _L1_attn_in['conv_k'], 'L1_attn_conv_v': _L1_attn_in['conv_v'], 'L1_attn_Wg': _L1_attn_in['Wg'], 'L1_attn_rms_weight': _L1_attn_in['rms_weight'], 'L1_attn_Wo': _L1_attn_in['Wo'], 'L1_ffn_router_w': _L1_ffn_in['router_w'], 'L1_ffn_w1': _L1_ffn_in['w1'], 'L1_ffn_b1': _L1_ffn_in['b1'], 'L1_ffn_w2': _L1_ffn_in['w2'], 'L1_ffn_b2': _L1_ffn_in['b2']}
    _x0 = _d['L0_attn_x']
    _d['L0_attn_x'] = jax.random.normal(jax.random.fold_in(jax.random.key(seed), 1), (16, 256, 128), dtype=_x0.dtype)
    del _x0
    return _d

def reference(L0_attn_x, L0_attn_w_qkv, L0_attn_w_out, L0_ffn_weight_fp8, L0_ffn_bias, L0_ffn_input_scale, L0_ffn_weight_scale, L1_attn_cos, L1_attn_sin, L1_attn_Wq, L1_attn_Wk, L1_attn_Wv, L1_attn_Wb, L1_attn_Wa, L1_attn_A_log, L1_attn_dt_bias, L1_attn_conv_q, L1_attn_conv_k, L1_attn_conv_v, L1_attn_Wg, L1_attn_rms_weight, L1_attn_Wo, L1_ffn_router_w, L1_ffn_w1, L1_ffn_b1, L1_ffn_w2, L1_ffn_b2):

    def _L0_attn_ref(x, w_qkv, w_out):
        import jax, jax.numpy as jnp
        import numpy as np
        B, S, D = (1, 512, 128)
        H, W = (16, 64)
        HD = D // H
        b, s, d = x.shape
        qkv = x @ w_qkv
        q, k, v = jnp.split(qkv, 3, axis=-1)
        to_heads = lambda t: t.reshape(b, s, H, HD).transpose(0, 2, 1, 3)
        q, k, v = map(to_heads, (q, k, v))
        C = s // W
        qc = q.reshape(b, H, C, W, HD)
        kc = k.reshape(b, H, C, W, HD)
        vc = v.reshape(b, H, C, W, HD)
        zero = jnp.zeros_like(kc[:, :, :1])
        k_prev = jnp.concatenate([zero, kc[:, :, :-1]], axis=2)
        v_prev = jnp.concatenate([jnp.zeros_like(vc[:, :, :1]), vc[:, :, :-1]], axis=2)
        kcat = jnp.concatenate([k_prev, kc], axis=3)
        vcat = jnp.concatenate([v_prev, vc], axis=3)
        scores = jnp.einsum('bhcqd,bhckd->bhcqk', qc, kcat) / HD ** 0.5
        wq = jnp.arange(W)
        jk = jnp.arange(2 * W)
        ci = jnp.arange(C)
        causal = wq[:, None] + W >= jk[None, :]
        valid = ci[:, None, None] * W + jk[None, None, :] - W >= 0
        mask = causal[None] & valid
        scores = jnp.where(mask[None, None], scores, -jnp.inf)
        attn = jax.nn.softmax(scores, axis=-1)
        out = jnp.einsum('bhcqk,bhckd->bhcqd', attn, vcat)
        out = out.reshape(b, H, s, HD).transpose(0, 2, 1, 3).reshape(b, s, d)
        return out @ w_out

    def _L0_ffn_ref(x, weight_fp8, bias, input_scale, weight_scale):
        import jax, jax.numpy as jnp
        import numpy as np
        FP8_MAX = 448.0
        x_q = jnp.clip(x / input_scale, -FP8_MAX, FP8_MAX)
        x_dq = x_q.astype(jnp.float8_e4m3fn).astype(x.dtype) * input_scale
        w_dq = weight_fp8 * weight_scale
        out = jnp.einsum('bsi,oi->bso', x_dq, w_dq) + bias
        return out

    def _L1_attn_ref(x, cos, sin, Wq, Wk, Wv, Wb, Wa, A_log, dt_bias, conv_q, conv_k, conv_v, Wg, rms_weight, Wo):
        import jax, jax.numpy as jnp
        import numpy as np
        B, T, D = (2, 256, 128)
        HEAD_DIM, N_HEADS, N_HH, HEAD_V_DIM, CONV_SIZE = (128, 8, 3, 128, 4)

        def _short_conv(x, w):
            cs = w.shape[-1]
            t = x.shape[1]
            xp = jnp.pad(x, ((0, 0), (cs - 1, 0), (0, 0)))
            y = sum((xp[:, i:i + t, :] * w[:, i] for i in range(cs)))
            return jax.nn.silu(y)

        def _l2norm(x, eps=1e-06):
            return x * jax.lax.rsqrt(jnp.sum(x * x, -1, keepdims=True) + eps)

        def _forward(x, Wq, Wk, Wv, Wb, Wa, A_log, dt_bias, conv_q, conv_k, conv_v, Wg, rms_weight, Wo):
            b, t, _ = x.shape
            h, d, dv, nh = (N_HEADS, HEAD_DIM, HEAD_V_DIM, N_HH)
            q = _short_conv(x @ Wq, conv_q).reshape(b, t, h, d)
            k = _short_conv(x @ Wk, conv_k).reshape(b, t, nh, h, d).transpose(0, 1, 3, 2, 4)
            v = _short_conv(x @ Wv, conv_v).reshape(b, t, nh, h, dv).transpose(0, 1, 3, 2, 4)
            beta = 2.0 * jax.nn.sigmoid(x @ Wb).reshape(b, t, nh, h).transpose(0, 1, 3, 2)
            g = -jnp.exp(A_log) * jax.nn.softplus(x @ Wa + dt_bias)
            q = _l2norm(q) * d ** (-0.5)
            k = _l2norm(k)

            def step(S, inp):
                qt, kt, vt, bt, gt = inp
                S = S * jnp.exp(gt)[..., None, None]
                for i in range(nh):
                    ki, vi, bi = (kt[:, :, i], vt[:, :, i], bt[:, :, i])
                    kS = jnp.einsum('bhd,bhde->bhe', ki, S)
                    S = S + bi[..., None, None] * (ki[..., None] * (vi - kS)[:, :, None, :])
                o = jnp.einsum('bhd,bhde->bhe', qt, S)
                return (S, o)
            xs = tuple((jnp.moveaxis(a, 1, 0) for a in (q, k, v, beta, g)))
            S0 = jnp.zeros((b, h, d, dv), x.dtype)
            _, o = jax.lax.scan(step, S0, xs)
            o = jnp.moveaxis(o, 0, 1)
            gate = (x @ Wg).reshape(b, t, h, dv)
            o = o * jax.lax.rsqrt(jnp.mean(o * o, -1, keepdims=True) + 1e-05) * rms_weight
            o = o * jax.nn.silu(gate)
            return o.reshape(b, t, h * dv) @ Wo
        return _forward(x, Wq, Wk, Wv, Wb, Wa, A_log, dt_bias, conv_q, conv_k, conv_v, Wg, rms_weight, Wo)

    def _L1_ffn_ref(hidden_states, router_w, w1, b1, w2, b2):
        import jax, jax.numpy as jnp
        import numpy as np
        TOP_K = 2
        x = hidden_states
        router_logits = jnp.einsum('bth,eh->bte', x, router_w)
        topk_values, topk_indices = jax.lax.top_k(router_logits, TOP_K)
        topk_weights = jax.nn.softmax(topk_values.astype(jnp.float32), axis=-1).astype(x.dtype)
        h1 = jnp.einsum('bth,efh->btef', x, w1) + b1
        h1 = jax.nn.gelu(h1, approximate=False)
        expert_outputs = jnp.einsum('btef,ehf->bteh', h1, w2) + b2
        gather_idx = topk_indices[..., None]
        topk_expert_outputs = jnp.take_along_axis(expert_outputs, gather_idx, axis=2)
        mixed_output = jnp.sum(topk_expert_outputs * topk_weights[..., None], axis=2)
        return mixed_output
    x = L0_attn_x
    xn = _layernorm(x, axis=-1)
    x = x + _L0_attn_ref(xn, L0_attn_w_qkv, L0_attn_w_out) + _L0_ffn_ref(xn, L0_ffn_weight_fp8, L0_ffn_bias, L0_ffn_input_scale, L0_ffn_weight_scale)
    xn = _layernorm(x, axis=-1)
    x = x + _L1_attn_ref(xn, L1_attn_cos, L1_attn_sin, L1_attn_Wq, L1_attn_Wk, L1_attn_Wv, L1_attn_Wb, L1_attn_Wa, L1_attn_A_log, L1_attn_dt_bias, L1_attn_conv_q, L1_attn_conv_k, L1_attn_conv_v, L1_attn_Wg, L1_attn_rms_weight, L1_attn_Wo) + _L1_ffn_ref(xn, L1_ffn_router_w, L1_ffn_w1, L1_ffn_b1, L1_ffn_w2, L1_ffn_b2)
    return x

_drawn_inputs = setup_inputs


def setup_inputs(seed=0):
    import zlib

    import numpy as np

    out = dict(_drawn_inputs(seed))
    spreads = {'L1_attn_rms_weight': (1.0, 0.6)}
    factors = {'L0_attn_w_qkv': 8.0,
     'L0_attn_w_out': 8.0,
     'L1_attn_Wq': 8.0,
     'L1_attn_Wk': 8.0,
     'L1_attn_Wv': 8.0,
     'L1_attn_Wb': 8.0,
     'L1_attn_Wa': 8.0,
     'L1_attn_A_log': 8.0,
     'L1_attn_dt_bias': 25.421,
     'L1_attn_conv_q': 8.0,
     'L1_attn_conv_k': 8.0,
     'L1_attn_conv_v': 8.0,
     'L1_attn_Wg': 8.0,
     'L1_attn_Wo': 8.0,
     'L1_ffn_router_w': 8.0,
     'L1_ffn_w1': 8.0,
     'L1_ffn_b1': 8.0,
     'L1_ffn_w2': 8.0,
     'L1_ffn_b2': 52.435}
    for name, (base, spread) in spreads.items():
        noise = np.random.default_rng([zlib.crc32(name.encode()), seed]).standard_normal(out[name].shape)
        drawn = base * np.exp(spread * noise) if base else spread * noise
        out[name] = jnp.asarray(drawn.astype(out[name].dtype))
    for name, factor in factors.items():
        out[name] = (out[name] * factor).astype(out[name].dtype)
    return out
```

```python
import concourse.bass as bass
from concourse import mybir
from contextlib import ExitStack

fp32 = mybir.dt.float32
i32 = mybir.dt.int32
u32 = mybir.dt.uint32
ALU = mybir.AluOpType
ACT = mybir.ActivationFunctionType
AX = mybir.AxisListType

P = 128
NB, T, D = 16, 256, 128
NTOK = NB * T
TT = T // P
NEG = -1.0e30
EPS = 1e-5


def now(n, k=1, per=1):
    return n * per + (k + 1)


def before(n, per=1):
    return n * per + 1


class Memory:

    def __init__(self, nc, ctx, phase):
        self.nc, self.ctx, self.phase, self.semaphores = nc, ctx, phase, []

    def sb(self, name, shape, dt=fp32):
        return self.ctx.enter_context(self.nc.sbuf_tensor(f"{self.phase}_{name}", shape, dt))

    def banks(self, count):
        return [self.ctx.enter_context(self.nc.psum_tensor(f"{self.phase}_bank{i}", [P, 512], fp32))
                for i in range(count)]

    def sem(self, name):
        s = self.nc.alloc_semaphore(f"{self.phase}_{name}")
        self.semaphores.append(s)
        return s

    def pair(self, name):
        return [self.sem(f"{name}{s}") for s in range(2)]


def end_phase(nc, m):
    nc.clear_and_free_semaphores(m.semaphores)
    nc.all_engine_barrier()


def local_attention_layer(nc, x, w_qkv, w_out, w_fp8_t, ffn_bias, in_scale, w_scale, x1_dram, xn2t_dram):
    H, HD, W = 16, 8, 64
    CAP = 448.0
    ROUNDS = [(0, 4 * r, 4, P) for r in range(4)] + [(1, 2 * r, 2, 3 * W) for r in range(8)]
    NR = len(ROUNDS)
    with ExitStack() as ctx:
        m = Memory(nc, ctx, "l0")
        wqkv = m.sb("wqkv", [P, 3 * D])
        wout = m.sb("wout", [P, D])
        w8 = m.sb("w8", [P, D])
        wdq = m.sb("wdq", [P, D])
        biasrow = m.sb("biasrow", [1, D])
        ones = m.sb("ones", [1, P])
        ident = m.sb("ident", [P, P])
        mask0 = m.sb("mask0", [P, P])
        mask1 = m.sb("mask1", [P, 3 * W])
        headmask = m.sb("headmask", [P, H])
        eps = m.sb("eps", [P, 1])
        s_in = m.sb("s_in", [P, 1])
        s_inv = m.sb("s_inv", [P, 1])
        s_w = m.sb("s_w", [P, 1])

        def two(name, shape, dt=fp32):
            return [m.sb(f"{name}{s}", shape, dt) for s in range(2)]

        xin = two("xin", [P, TT, D])
        stats = two("stats", [P, TT, 6])
        mv = two("mv", [P, TT, 2])
        lnv = two("lnv", [P, TT])
        rstd0 = two("rstd0", [P, TT])
        rr = two("rr", [P, TT])
        rv = two("rv", [P, TT])
        rstd = two("rstd", [P, TT])
        xnq = two("xnq", [P, 2 * TT, D])
        ebits = two("ebits", [P, TT, D])
        xT = two("xT", [P, 2 * TT, P])
        qT = two("qT", [P, T])
        kT = two("kT", [P, T])
        kTm = two("kTm", [P, H, T])
        vaug = two("vaug", [P, 3, H, HD + 1])
        mx = two("mx", [P, 2, 4])
        pr = two("pr", [P, 2, 512])
        pT = two("pT", [P, 2, 512])
        rden = two("rden", [P, TT, H])
        attn = two("attn", [P, TT, D])
        attnT = two("attnT", [P, TT, P])
        x1 = two("x1", [P, TT, D])
        xn2 = two("xn2", [P, TT, D])
        xn2T = two("xn2T", [P, T])
        bank = m.banks(8)
        bk = [bank[0:4], bank[4:8]]

        weights_in = m.sem("weights_in")
        const_step = m.sem("const_step")
        const_done = m.sem("const_done")
        wdq_done = m.sem("wdq_done")
        names = ("x_loaded x_norm_read stats_done var_done ln_done rstd0_done sq_done sv_done half_done rstd_done "
                 "xn_done xs_done xc_done eb_done magic_done up_done down_done xq_done "
                 "xT_psum xT_done qk_psum v_psum qT_done kT_done v_done kTm_done "
                 "scores max_done shifted probs probsT pT_done av_done rden_done attn_done "
                 "attnT_psum attnT_done out_psum x1_done xn2_done xn2T_psum xn2T_done").split()
        S = {k: m.pair(k) for k in names}
        x1_stored = m.pair("x1_stored")
        xn2T_stored = m.pair("xn2T_stored")
        carrier = m.sem("carrier")
        LOOPS = NB // 2
        block = ctx.enter_context(nc.Block())

        @block.sync
        def _(sp):
            for s in m.semaphores[4:]:
                sp.sem_inc(s, 1)
            with nc.allow_non_contiguous_dma(reason="small broadcasts"):
                sp.dma_start(wqkv[:], w_qkv).then_inc(weights_in, 16)
                sp.dma_start(wout[:], w_out).then_inc(weights_in, 16)
                sp.dma_start(w8[:], w_fp8_t).then_inc(weights_in, 16)
                sp.dma_start(biasrow[:], ffn_bias).then_inc(weights_in, 16)
                sp.dma_start(s_in[:], in_scale.broadcast_to([P, 1])).then_inc(weights_in, 16)
                sp.dma_start(s_w[:], w_scale.broadcast_to([P, 1])).then_inc(weights_in, 16)
            with sp.Fori(0, LOOPS) as n:
                tok = [sp.snap((n * 2 + s) * T) for s in range(2)]
                for s in range(2):
                    sp.wait_ge(S["x1_done"][s], before(n, TT))
                    sp.sem_inc(carrier, 1)
                    sp.dma_start(xin[s][:], x[bass.ds(tok[s], T), :].rearrange("(t p) d -> p t d", p=P)).then_inc(S["x_loaded"][s], 16)
                for s in range(2):
                    sp.wait_ge(S["x1_done"][s], now(n, TT, TT))
                    sp.sem_inc(carrier, 1)
                    sp.dma_start(x1_dram[bass.ds(tok[s], T), :].rearrange("(t p) d -> p t d", p=P), x1[s][:]).then_inc(x1_stored[s], 16)
                    sp.wait_ge(S["xn2T_done"][s], now(n))
                    sp.sem_inc(carrier, 1)
                    sp.dma_start(xn2t_dram[:, bass.ds(tok[s], T)], xn2T[s][:]).then_inc(xn2T_stored[s], 16)
            for s in range(2):
                sp.wait_ge(x1_stored[s], 16 * LOOPS + 1)
                sp.wait_ge(xn2T_stored[s], 16 * LOOPS + 1)

        @block.gpsimd
        def _(pool):
            pool.memset(ident[:], 0.0).then_inc(const_step, 1)
            pool.memset(mask0[:], 0.0).then_inc(const_step, 1)
            pool.memset(mask1[:], 0.0).then_inc(const_step, 1)
            pool.memset(headmask[:], 1.0).then_inc(const_step, 1)
            pool.memset(eps[:], EPS).then_inc(const_done, 1)
            pool.memset(ones[:], 1.0).then_inc(const_done, 1)
            for s in range(2):
                pool.memset(vaug[s][:], 1.0).then_inc(const_done, 1)
            pool.wait_ge(const_step, 4)
            pool.affine_select(out=ident[:], in_=ident[:], compare_op=ALU.not_equal, fill=1.0, base=0,
                               pattern=[[-1, P]], channel_multiplier=1).then_inc(const_done, 1)
            pool.affine_select(out=mask0[:], in_=mask0[:], compare_op=ALU.is_ge, fill=NEG, base=0,
                               pattern=[[-1, P]], channel_multiplier=1).then_inc(const_done, 1)
            pool.affine_select(out=mask1[:], in_=mask1[:], compare_op=ALU.is_ge, fill=NEG, base=W,
                               pattern=[[-1, 3 * W]], channel_multiplier=1).then_inc(const_step, 1)
            pool.affine_select(out=headmask[:], in_=headmask[:], compare_op=ALU.is_ge, fill=0.0, base=0,
                               pattern=[[-HD, H]], channel_multiplier=1).then_inc(const_step, 1)
            pool.wait_ge(const_step, 6)
            pool.memset(mask1[W:P, 0:W], NEG).then_inc(const_step, 1)
            pool.wait_ge(const_step, 7)
            pool.affine_select(out=headmask[:], in_=headmask[:], compare_op=ALU.is_ge, fill=0.0, base=HD - 1,
                               pattern=[[HD, H]], channel_multiplier=-1).then_inc(const_done, 1)
        CONSTS = 7

        @block.scalar
        def _(act):
            def rsqrt_seed(s, n, k):
                act.wait_ge(S["var_done"][s], now(n, k, 2))
                if k == 2:
                    act.wait_ge(S["half_done"][s], now(n, 1, 2))
                act.activation(lnv[s][:], mv[s][:, :, 1], ACT.Ln, bias=eps[:, 0:1]).then_inc(S["ln_done"][s], 1)
                act.wait_ge(S["ln_done"][s], now(n, k, 2))
                act.activation(rstd0[s][:], lnv[s][:], ACT.Exp, scale=-0.5).then_inc(S["rstd0_done"][s], 1)

            act.wait_ge(const_done, CONSTS)
            act.preload_act_table_set("natural_log_exp_and_others")
            with act.Fori(0, LOOPS) as n:
                for s in range(2):
                    rsqrt_seed(s, n, 1)
                for s in range(2):
                    act.wait_ge(S["xT_psum"][s], now(n))
                    act.activation(xT[s][:], bk[s][0][:].rearrange("p (a b) -> p a b", b=P), ACT.Copy).then_inc(S["xT_done"][s], 1)
                for s in range(2):
                    act.wait_ge(S["qk_psum"][s], now(n))
                    act.wait_ge(S["scores"][s], before(n, NR))
                    act.activation(qT[s][:], bk[s][1][:, 0:T], ACT.Copy, scale=float(HD) ** -0.5).then_inc(S["qT_done"][s], 1)
                    act.wait_ge(S["kTm_done"][s], before(n))
                    act.activation(kT[s][:], bk[s][1][:, T:2 * T], ACT.Copy).then_inc(S["kT_done"][s], 1)
                    act.wait_ge(S["v_psum"][s], now(n))
                    act.wait_ge(S["av_done"][s], before(n, NR))
                    act.activation(vaug[s][:, 0:2, :, 0:HD],
                                   bk[s][2][:, 0:2 * D].rearrange("p (v h e) -> p v h e", v=2, e=HD), ACT.Copy).then_inc(S["v_done"][s], 1)
                    act.activation(vaug[s][0:W, 2, :, 0:HD],
                                   bk[s][2][0:W, 2 * D:3 * D].rearrange("p (h e) -> p h e", e=HD), ACT.Copy).then_inc(S["v_done"][s], 1)

                def probabilities(s, r):
                    w, h0, hb, nk = ROUNDS[r]
                    act.wait_ge(S["shifted"][s], now(n, r + 1, NR))
                    act.activation(pr[s][:, r % 2, 0:hb * nk], pr[s][:, r % 2, 0:hb * nk], ACT.Exp).then_inc(S["probs"][s], 1)

                def probabilities_T(s, r):
                    w, h0, hb, nk = ROUNDS[r]
                    act.wait_ge(S["probsT"][s], now(n, r + 1, NR))
                    if r >= 2:
                        act.wait_ge(S["av_done"][s], now(n, r - 1, NR))
                    if w == 0:
                        act.activation(pT[s][:, r % 2, :], bk[s][2][:], ACT.Copy).then_inc(S["pT_done"][s], 2)
                    else:
                        act.activation(pT[s][:, r % 2, 0:2 * P], bk[s][2][:, 0:2 * P], ACT.Copy).then_inc(S["pT_done"][s], 1)
                        act.activation(pT[s][0:W, r % 2, 2 * P:4 * P], bk[s][2][0:W, 2 * P:4 * P], ACT.Copy).then_inc(S["pT_done"][s], 1)

                for s in range(2):
                    probabilities(s, 0)
                for r in range(NR):
                    for s in range(2):
                        if r + 1 < NR:
                            probabilities(s, r + 1)
                        probabilities_T(s, r)
                for s in range(2):
                    act.wait_ge(S["attnT_psum"][s], now(n))
                    act.activation(attnT[s][:], bk[s][0][:, 0:T].rearrange("p (a b) -> p a b", b=P), ACT.Copy).then_inc(S["attnT_done"][s], 1)
                for s in range(2):
                    rsqrt_seed(s, n, 2)
                for s in range(2):
                    act.wait_ge(S["xn2T_psum"][s], now(n))
                    act.wait_ge(xn2T_stored[s], before(n, 16))
                    act.activation(xn2T[s][:], bk[s][2][:, 0:T], ACT.Copy).then_inc(S["xn2T_done"][s], 1)

        @block.vector
        def _(dve):
            dve.wait_ge(weights_in, 96)
            dve.reciprocal(s_inv[:], s_in[:]).then_inc(wdq_done, 1)
            dve.tensor_scalar(wdq[:], w8[:], s_w[:, 0:1], None, ALU.mult).then_inc(wdq_done, 1)
            dve.wait_ge(const_done, CONSTS)
            dve.wait_ge(wdq_done, 2)

            def moments(s, n, src, k):
                if k == 2:
                    dve.wait_ge(S["xn_done"][s], now(n, TT, TT))
                for t in range(TT):
                    dve.bn_stats(stats[s][:, t, :], src[s][:, t, :]).then_inc(S["stats_done"][s], 1)
                dve.wait_ge(S["stats_done"][s], now(n, TT * k, 2 * TT))
                dve.sem_inc(carrier, 1)
                for t in range(TT):
                    ins = dve.bn_aggr(mv[s][:, t, :], stats[s][:, t, :])
                ins.then_inc(S["var_done"][s], 1)

            def sharpen(s, n, k):
                dve.wait_ge(S["rstd0_done"][s], now(n, k, 2))
                dve.tensor_tensor(rr[s][:], rstd0[s][:], rstd0[s][:], ALU.mult).then_inc(S["sq_done"][s], 1)
                dve.wait_ge(S["sq_done"][s], now(n, k, 2))
                dve.scalar_tensor_tensor(out=rv[s][:], in0=mv[s][:, :, 1], scalar=eps[:, 0:1], in1=rr[s][:],
                                         op0=ALU.add, op1=ALU.mult).then_inc(S["sv_done"][s], 1)
                dve.wait_ge(S["sv_done"][s], now(n, k, 2))
                dve.tensor_scalar(rr[s][:], rv[s][:], -0.5, 1.5, ALU.mult, ALU.add).then_inc(S["half_done"][s], 1)
                dve.wait_ge(S["half_done"][s], now(n, k, 2))
                dve.tensor_tensor(rstd[s][:], rstd0[s][:], rr[s][:], ALU.mult).then_inc(S["rstd_done"][s], 1)
                dve.wait_ge(S["rstd_done"][s], now(n, k, 2))

            with dve.Fori(0, LOOPS) as n:
                for s in range(2):
                    dve.wait_ge(S["x_loaded"][s], now(n, 16, 16))
                    moments(s, n, xin, 1)
                for s in range(2):
                    sharpen(s, n, 1)
                    dve.wait_ge(S["xT_psum"][s], before(n))
                    for t in range(TT):
                        dve.tensor_scalar(xnq[s][:, t, :], xin[s][:, t, :], mv[s][:, t, 0:1], rstd[s][:, t:t + 1],
                                          ALU.subtract, ALU.mult).then_inc(S["xn_done"][s], 1)
                for s in range(2):
                    q = xnq[s][:, TT:2 * TT, :]
                    dve.wait_ge(S["xn_done"][s], now(n, TT, TT))
                    dve.tensor_scalar(q, xnq[s][:, 0:TT, :], s_inv[:, 0:1], CAP, ALU.mult, ALU.min).then_inc(S["xs_done"][s], 1)
                for s in range(2):
                    q = xnq[s][:, TT:2 * TT, :]
                    dve.wait_ge(S["xs_done"][s], now(n))
                    dve.tensor_scalar(q, q, -CAP, None, ALU.max).then_inc(S["xc_done"][s], 1)
                for s in range(2):
                    q = xnq[s][:, TT:2 * TT, :]
                    dve.wait_ge(S["xc_done"][s], now(n))
                    dve.tensor_scalar(ebits[s][:].bitcast(i32), q.bitcast(i32), 0x7F800000, None, ALU.bitwise_and).then_inc(S["eb_done"][s], 1)
                for s in range(2):
                    dve.wait_ge(S["eb_done"][s], now(n))
                    dve.tensor_scalar(ebits[s][:], ebits[s][:], 2.0 ** -6, 1.5 * 2.0 ** 20, ALU.max, ALU.mult).then_inc(S["magic_done"][s], 1)
                for s in range(2):
                    q = xnq[s][:, TT:2 * TT, :]
                    dve.wait_ge(S["magic_done"][s], now(n))
                    dve.tensor_tensor(q, q, ebits[s][:], ALU.add).then_inc(S["up_done"][s], 1)
                for s in range(2):
                    q = xnq[s][:, TT:2 * TT, :]
                    dve.wait_ge(S["up_done"][s], now(n))
                    dve.tensor_tensor(q, q, ebits[s][:], ALU.subtract).then_inc(S["down_done"][s], 1)
                for s in range(2):
                    q = xnq[s][:, TT:2 * TT, :]
                    dve.wait_ge(S["down_done"][s], now(n))
                    dve.tensor_scalar(q, q, s_in[:, 0:1], None, ALU.mult).then_inc(S["xq_done"][s], 1)
                for s in range(2):
                    dve.wait_ge(S["kT_done"][s], now(n))
                    dve.wait_ge(S["scores"][s], before(n, NR))
                    for h in range(H):
                        ins = dve.tensor_scalar(kTm[s][:, h, :], kT[s][:], headmask[:, h:h + 1], None, ALU.mult)
                    ins.then_inc(S["kTm_done"][s], 1)
                for r, (w, h0, hb, nk) in enumerate(ROUNDS):
                    for s in range(2):
                        sc = bk[s][r % 2][:, 0:hb * nk].rearrange("p (h k) -> p h k", k=nk)
                        dve.wait_ge(S["scores"][s], now(n, r + 1, NR))
                        dve.tensor_reduce(mx[s][:, r % 2, 0:hb], sc, AX.X, ALU.max).then_inc(S["max_done"][s], 1)
                    for s in range(2):
                        sc = bk[s][r % 2][:, 0:hb * nk].rearrange("p (h k) -> p h k", k=nk)
                        dve.wait_ge(S["max_done"][s], now(n, r + 1, NR))
                        if r >= 2:
                            dve.wait_ge(S["probsT"][s], now(n, r - 1, NR))
                        dve.tensor_tensor(pr[s][:, r % 2, 0:hb * nk].rearrange("p (h k) -> p h k", k=nk), sc,
                                          mx[s][:, r % 2, 0:hb].unsqueeze(2).broadcast_to([P, hb, nk]),
                                          ALU.subtract).then_inc(S["shifted"][s], 1)
                for s in range(2):
                    ao = bk[s][3][:, 0:TT * H * (HD + 1)].rearrange("p (w h e) -> p w h e", w=TT, e=HD + 1)
                    dve.wait_ge(S["av_done"][s], now(n, NR, NR))
                    dve.reciprocal(rden[s][:], ao[:, :, :, HD]).then_inc(S["rden_done"][s], 1)
                for s in range(2):
                    ao = bk[s][3][:, 0:TT * H * (HD + 1)].rearrange("p (w h e) -> p w h e", w=TT, e=HD + 1)
                    dve.wait_ge(S["rden_done"][s], now(n))
                    for w in range(TT):
                        dve.tensor_tensor(attn[s][:, w, :].rearrange("p (h e) -> p h e", e=HD), ao[:, w, :, 0:HD],
                                          rden[s][:, w, :].unsqueeze(2).broadcast_to([P, H, HD]), ALU.mult).then_inc(S["attn_done"][s], 1)
                for s in range(2):
                    dve.wait_ge(S["out_psum"][s], now(n))
                    dve.wait_ge(x1_stored[s], before(n, 16))
                    for t in range(TT):
                        dve.tensor_tensor(x1[s][:, t, :], xin[s][:, t, :], bk[s][1][:, t * D:(t + 1) * D], ALU.add).then_inc(S["x1_done"][s], 1)
                for s in range(2):
                    dve.wait_ge(S["x1_done"][s], now(n, TT, TT))
                    moments(s, n, x1, 2)
                for s in range(2):
                    sharpen(s, n, 2)
                    for t in range(TT):
                        dve.tensor_scalar(xn2[s][:, t, :], x1[s][:, t, :], mv[s][:, t, 0:1], rstd[s][:, t:t + 1],
                                          ALU.subtract, ALU.mult).then_inc(S["xn2_done"][s], 1)

        @block.tensor
        def _(pe):
            pe.wait_ge(weights_in, 96)
            pe.wait_ge(const_done, CONSTS)
            pe.wait_ge(wdq_done, 2)
            with pe.Fori(0, LOOPS) as n:
                for s in range(2):
                    pe.wait_ge(S["xq_done"][s], now(n))
                    for t in range(2 * TT):
                        ins = pe.transpose(bk[s][0][:, t * P:(t + 1) * P], xnq[s][:, t, :], ident[:])
                    ins.then_inc(S["xT_psum"][s], 1)
                for s in range(2):
                    xnT = xT[s][:, 0:TT, :].rearrange("p t q -> p (t q)")
                    pe.wait_ge(S["xT_done"][s], now(n))
                    pe.matmul(bk[s][1][:, 0:T], wqkv[:, 0:D], xnT, start=True, stop=True)
                    pe.matmul(bk[s][1][:, T:2 * T], wqkv[:, D:2 * D], xnT, start=True, stop=True).then_inc(S["qk_psum"][s], 1)
                    pe.wait_ge(S["xn2T_done"][s], before(n))
                    for v, (k0, rows) in enumerate(((0, P), (W, P), (3 * W, W))):
                        ins = pe.matmul(bk[s][2][0:rows, v * D:(v + 1) * D], xnT[:, k0:k0 + rows], wqkv[:, 2 * D:3 * D],
                                        start=True, stop=True)
                    ins.then_inc(S["v_psum"][s], 1)

                def scores(s, r):
                    w, h0, hb, nk = ROUNDS[r]
                    k0 = w * W
                    out = bk[s][r % 2][:, 0:hb * nk].rearrange("p (h k) -> p h k", k=nk)
                    if r == 0:
                        pe.wait_ge(S["qT_done"][s], now(n))
                        pe.wait_ge(S["kTm_done"][s], now(n))
                    if r >= 2:
                        pe.wait_ge(S["shifted"][s], now(n, r - 1, NR))
                    pe.matmul(out, qT[s][:, w * P:(w + 1) * P], kTm[s][:, h0:h0 + hb, k0:k0 + nk], start=True, stop=False)
                    mask = (mask0 if w == 0 else mask1)[:].unsqueeze(1).broadcast_to([P, hb, nk])
                    pe.matmul(out, ident[:], mask, start=False, stop=True).then_inc(S["scores"][s], 1)

                def transposes(s, r):
                    w, h0, hb, nk = ROUNDS[r]
                    pe.wait_ge(S["probs"][s], now(n, r + 1, NR))
                    if r == 0:
                        pe.wait_ge(S["v_done"][s], now(n, 2, 2))
                    else:
                        pe.wait_ge(S["pT_done"][s], now(n, 2 * r, 2 * NR))
                    for h in range(hb):
                        ins = pe.transpose(bk[s][2][:, h * P:(h + 1) * P], pr[s][:, r % 2, h * nk:h * nk + P], ident[:])
                    if w == 1:
                        for h in range(hb):
                            ins = pe.transpose(bk[s][2][0:W, (2 + h) * P:(3 + h) * P], pr[s][:, r % 2, h * nk + P:(h + 1) * nk], ident[:])
                    ins.then_inc(S["probsT"][s], 1)

                def values(s, r):
                    w, h0, hb, nk = ROUNDS[r]
                    pe.wait_ge(S["pT_done"][s], now(n, 2 * r + 2, 2 * NR))
                    if r == 0:
                        pe.wait_ge(S["attn_done"][s], before(n, TT))
                    for h in range(hb):
                        c = (w * H + h0 + h) * (HD + 1)
                        out = bk[s][3][:, c:c + HD + 1]
                        ins = pe.matmul(out, pT[s][:, r % 2, h * P:(h + 1) * P], vaug[s][:, w, h0 + h, :], start=True, stop=w == 0)
                        if w == 1:
                            ins = pe.matmul(out, pT[s][0:W, r % 2, (2 + h) * P:(3 + h) * P], vaug[s][0:W, 2, h0 + h, :], start=False, stop=True)
                    ins.then_inc(S["av_done"][s], 1)

                for r in range(NR + 1):
                    for s in range(2):
                        if r < NR:
                            scores(s, r)
                    for s in range(2):
                        if r >= 1:
                            transposes(s, r - 1)
                    for s in range(2):
                        if r >= 1:
                            values(s, r - 1)
                for s in range(2):
                    pe.wait_ge(S["attn_done"][s], now(n, TT, TT))
                    pe.wait_ge(S["shifted"][s], now(n, NR, NR))
                    for t in range(TT):
                        ins = pe.transpose(bk[s][0][:, t * P:(t + 1) * P], attn[s][:, t, :], ident[:])
                    ins.then_inc(S["attnT_psum"][s], 1)
                for s in range(2):
                    pe.wait_ge(S["attnT_done"][s], now(n))
                    for t in range(TT):
                        out = bk[s][1][:, t * D:(t + 1) * D]
                        pe.matmul(out, attnT[s][:, t, :], wout[:], start=True, stop=False)
                        pe.matmul(out, xT[s][:, TT + t, :], wdq[:], start=False, stop=False)
                        ins = pe.matmul(out, ones[:], biasrow[:], start=False, stop=True)
                    ins.then_inc(S["out_psum"][s], 1)
                for s in range(2):
                    pe.wait_ge(S["xn2_done"][s], now(n, TT, TT))
                    pe.wait_ge(S["pT_done"][s], now(n, 2 * NR, 2 * NR))
                    for t in range(TT):
                        ins = pe.transpose(bk[s][2][:, t * P:(t + 1) * P], xn2[s][:, t, :], ident[:])
                    ins.then_inc(S["xn2T_psum"][s], 1)
    end_phase(nc, m)


def delta_attention_layer(nc, x1_dram, xn2t_dram, w_proj, conv_w, w_beta, w_decay, a_log, dt_bias, rms_w, w_o, x2_dram):
    H, NH, C, GH, DV = 8, 3, 32, 4, 128
    R = NH * C
    NC = T // C
    BIG = 2.0 ** 14
    NQ, NK, NV = H, NH * H, NH * H
    NCONV = NQ + NK + NV
    TAPS = 4
    LEVELS = 7
    FH = [C, 2 * C] + [R // 2] * 5
    QEPS, OEPS = 1e-6, 1e-5
    ATANH = [1.0 / (2 * j + 1) for j in range(8)]
    with ExitStack() as ctx:
        m = Memory(nc, ctx, "l1")
        wp = m.sb("wp", [P, (NCONV + H) * P])
        wo = m.sb("wo", [P, H, D])
        wb = m.sb("wb", [P, NK])
        wa = m.sb("wa", [P, H])
        cw = m.sb("cw", [P, NCONV, TAPS])
        alog = m.sb("alog", [C, H])
        expa = m.sb("expa", [C, H])
        dtb = m.sb("dtb", [C, H])
        rmsw = m.sb("rmsw", [P, 1])
        ident = m.sb("ident", [P, P])
        ones = m.sb("ones", [P, P])
        mean_dv = m.sb("mean_dv", [P, P])
        mean_eps = m.sb("mean_eps", [P, P])
        qeps = m.sb("qeps", [P, 1])
        oeps = m.sb("oeps", [P, 1])
        ranksel = m.sb("ranksel", [R, NH])
        later = m.sb("later", [P, R])
        later_only = m.sb("later_only", [C, P])
        upto = m.sb("upto", [C, P])
        block_mask = m.sb("block_mask", [R, LEVELS, 2 * C])
        xb = m.sb("xb", [P, T])
        xb3 = m.sb("xb3", [P, T, NH])
        y = m.sb("y", [P, NCONV, T])
        gate = m.sb("gate", [P, H, T])
        og = m.sb("og", [P, H, T])
        x1 = m.sb("x1", [P, TT, D])
        x2 = m.sb("x2", [P, TT, D])
        beta_t = m.sb("beta_t", [R, NC, NH, H])
        beta_s = m.sb("beta_s", [R, NC, NH, H])
        beta = m.sb("beta", [R, NC, H])
        z = m.sb("z", [C, NC, H])
        az = m.sb("az", [C, NC, H])
        zp = m.sb("zp", [C, NC, H])
        ez = m.sb("ez", [C, NC, H])
        ez2 = m.sb("ez2", [C, NC, H])
        ezr = m.sb("ezr", [C, NC, H])
        sz = m.sb("sz", [C, NC, H])
        sz2 = m.sb("sz2", [C, NC, H])
        poly = m.sb("poly", [C, NC, H])
        g = m.sb("g", [C, NC, H])
        decays = m.sb("decays", [P, 3, NC, H])

        def two(name, shape):
            return [m.sb(f"{name}{s}", shape) for s in range(2)]

        kq = two("kq", [P, GH, P])
        vt = two("vt", [P, GH, R])
        sq = two("sq", [P, GH, P])
        gr = two("gr", [P, GH, P])
        ex = two("ex", [R, GH, P])
        at = two("at", [R, GH, P])
        lnss = two("lnss", [R, GH])
        vlen = two("vlen", [R, GH])
        sse = two("sse", [R, GH])
        inv = two("inv", [R, GH])
        bp = two("bp", [R, GH])
        M = two("M", [R, GH, R])
        MT = two("MT", [R, GH, R])
        pl = two("pl", [R, GH, 2 * C])
        kd = two("kd", [R, GH, P])
        vn = two("vn", [R, GH, DV])
        ksg = two("ksg", [P, GH, DV])
        rhs = two("rhs", [R, GH, DV])
        w = two("w", [R, GH, DV])
        st = two("st", [P, GH, DV])
        st_dec = two("st_dec", [P, GH, DV])
        ot = two("ot", [P, GH, C])
        osq = two("osq", [P, GH, C])
        lnf = two("lnf", [P, GH, C])
        fac = two("fac", [P, GH, C])
        otf = two("otf", [P, GH, C])
        bank = m.banks(8)
        bk = [bank[0:4], bank[4:8]]

        weights_in = m.sem("weights_in")
        const_step = m.sem("const_step")
        const_done = m.sem("const_done")
        expa_done = m.sem("expa_done")
        gr_init = m.sem("gr_init")
        UNPRIMED = len(m.semaphores)
        seq = {k: m.sem(k) for k in ("xb_loaded xb3_done proj tap0 taps_done silu_done gate_done gatew_done "
                                     "bg_psum tanh_done beta1_done betas_done beta_done z_done abs_done exp_z plus2 recip_z s_done s2_done "
                                     "tap_step horner softplus decay_in g_done decay_psum decay_done "
                                     "wo_psum x1_loaded x2_done x2_stored st_zero").split()}
        S = {k: m.pair(k) for k in ("kq_done v_done sq_done gr_done gram e_psum ss_psum ex_done at_done ln_done vlen_done "
                                    "sse_done inv_done bp_done m0_done p_psum p_done m_psum m_done t_psum t_done "
                                    "kt_psum kd_done vt_psum vn_done ks_psum ksg_done rhs_done u_psum w_done dec_done su_psum st_done "
                                    "o_psum o_done osq_done rms_psum lnf_done fac_done otf_done og_done").split()}
        carrier = m.sem("carrier")
        block = ctx.enter_context(nc.Block())

        def fh(t, l):
            if l < 2:
                return t.rearrange("p h (t i) -> p h t i", i=NH)[:, :, :, 0:l + 1]
            w_ = NH << (l - 2)
            return t.rearrange("p h (b two m) -> p h b two m", two=2, m=w_)[:, :, :, 0, :]

        def compact(t, l):
            n = l + 1 if l < 2 else NH << (l - 2)
            return t[:, :, 0:FH[l]].rearrange("p h (b m) -> p h b m", m=n)

        @block.sync
        def _(sp):
            for s in m.semaphores[UNPRIMED:]:
                sp.sem_inc(s, 1)
            with nc.allow_non_contiguous_dma(reason="small broadcasts"):
                sp.dma_start(wp[:], w_proj).then_inc(weights_in, 16)
                sp.dma_start(cw[:], conv_w).then_inc(weights_in, 16)
                sp.dma_start(wo[:], w_o).then_inc(weights_in, 16)
                sp.dma_start(wb[:], w_beta).then_inc(weights_in, 16)
                sp.dma_start(wa[:], w_decay).then_inc(weights_in, 16)
                sp.dma_start(alog[:], a_log.broadcast_to([C, H])).then_inc(weights_in, 16)
                sp.dma_start(dtb[:], dt_bias.broadcast_to([C, H])).then_inc(weights_in, 16)
                sp.dma_start(rmsw[:], rms_w).then_inc(weights_in, 16)
            with sp.Fori(0, NB) as b:
                tok = sp.snap(b * T)
                sp.wait_ge(seq["bg_psum"], before(b))
                sp.sem_inc(carrier, 1)
                sp.dma_start(xb[:], xn2t_dram[:, bass.ds(tok, T)]).then_inc(seq["xb_loaded"], 16)
                sp.wait_ge(seq["x2_done"], before(b))
                sp.sem_inc(carrier, 1)
                sp.dma_start(x1[:], x1_dram[bass.ds(tok, T), :].rearrange("(t p) d -> p t d", p=P)).then_inc(seq["x1_loaded"], 16)
                sp.wait_ge(seq["x2_done"], now(b))
                sp.sem_inc(carrier, 1)
                sp.dma_start(x2_dram[bass.ds(tok, T), :].rearrange("(t p) d -> p t d", p=P), x2[:]).then_inc(seq["x2_stored"], 16)
            sp.wait_ge(seq["x2_stored"], 16 * NB + 1)

        @block.gpsimd
        def _(pool):
            step = [0]

            def const(ins):
                step[0] += 1
                ins.then_inc(const_step, 1)
                pool.wait_ge(const_step, step[0])

            def select(t, pattern, base, ch, op=ALU.is_ge, fill=0.0):
                const(pool.affine_select(out=t, in_=t, compare_op=op, fill=fill, base=base, pattern=pattern, channel_multiplier=ch))

            const(pool.memset(ones[:], 1.0))
            const(pool.memset(mean_dv[:], 1.0 / DV))
            const(pool.memset(mean_eps[:], OEPS * DV))
            const(pool.memset(qeps[:], QEPS))
            const(pool.memset(oeps[:], OEPS * DV * QEPS))
            const(pool.memset(ident[:], 0.0))
            select(ident[:], [[-1, P]], 0, 1, ALU.not_equal, 1.0)
            const(pool.memset(ranksel[:], 0.0))
            for t in range(C):
                select(ranksel[:], [[-1, NH]], -NH * t, 1, ALU.not_equal, 1.0)
            const(pool.memset(later[:], 0.0))
            select(later[:], [[-1, R]], -C, 1, ALU.not_equal, 1.0)
            const(pool.memset(later[0:C, :], 1.0))
            select(later[0:C, :].rearrange("p (t i) -> p t i", i=NH), [[-1, C], [0, NH]], -1, 1)
            const(pool.memset(later_only[:], 0.0))
            const(pool.tensor_copy(later_only[:, 0:R], later[0:C, :]))
            const(pool.memset(upto[:], 1.0))
            select(upto[:, 0:R].rearrange("p (t i) -> p t i", i=NH), [[1, C], [0, NH]], 0, -1)
            select(upto[:, R:P], [[1, C]], 0, -1)
            const(pool.memset(block_mask[:], -1.0))
            for l in range(2):
                bm = block_mask[:, l, 0:FH[l]].rearrange("p (t i) -> p t i", i=l + 1)
                select(bm, [[-NH, C], [0, l + 1]], -(l + 1), 1, ALU.is_equal)
            for l in range(2, LEVELS):
                w_ = NH << (l - 2)
                bm = block_mask[:, l, 0:FH[l]].rearrange("p (b m) -> p b m", m=w_)
                select(bm, [[-2 * w_, FH[l] // w_], [0, w_]], -w_, 1)
                select(bm, [[2 * w_, FH[l] // w_], [0, w_]], 2 * w_ - 1, -1)
            for s in range(2):
                const(pool.memset(gr[s][:], -BIG))
                select(gr[s][:, :, 0:R], [[0, GH], [-1, R]], -C, 1)
                select(gr[s][:, :, R:P], [[0, GH], [-NH, C]], -C - NH, 1)
                const(pool.memset(at[s][:], 0.0))
            pool.drain().then_inc(const_done, 1)

            with pool.Fori(0, NB) as b:
                for s in range(2):
                    pool.wait_ge(S["st_done"][s], before(b, NC))
                    pool.wait_ge(S["dec_done"][s], before(b, NC))
                    pool.sem_inc(carrier, 1)
                    pool.memset(st[s][:], 0.0).then_inc(seq["st_zero"], 1)
                pool.wait_ge(seq["decay_done"], now(b))
                pool.sem_inc(carrier, 1)
                with pool.Fori(0, NC) as c:
                    n = b * NC + c
                    for s in range(2):
                        pool.wait_ge(S["e_psum"][s], before(n))
                        pool.tensor_tensor(gr[s][0:C, :, :], upto[:].unsqueeze(1).broadcast_to([C, GH, P]),
                                           g[:, bass.ds(c, 1), s * GH:(s + 1) * GH].rearrange("p a h -> p (a h)").unsqueeze(2).broadcast_to([C, GH, P]),
                                           ALU.mult).then_inc(S["gr_done"][s], 1)
                    for s in range(2):
                        pool.wait_ge(S["bp_done"][s], now(n))
                        pool.wait_ge(S["u_psum"][s], before(n))
                        pool.tensor_tensor(M[s][:], ident[0:R, 0:R].unsqueeze(1).broadcast_to([R, GH, R]),
                                           bp[s][:].unsqueeze(2).broadcast_to([R, GH, R]), ALU.mult).then_inc(S["m0_done"][s], 1)
                    for s in range(2):
                        if s == 0:
                            pool.wait_ge(seq["st_zero"], now(b, 2, 2))
                        pool.wait_ge(S["st_done"][s], before(n))
                        pool.tensor_tensor(st_dec[s][:], st[s][:],
                                           decays[:, 2, bass.ds(c, 1), s * GH:(s + 1) * GH].rearrange("p a h -> p (a h)").unsqueeze(2).broadcast_to([P, GH, DV]),
                                           ALU.mult).then_inc(S["dec_done"][s], 1)
                    for s in range(2):
                        pool.wait_ge(S["ksg_done"][s], now(n))
                        pool.wait_ge(S["vn_done"][s], now(n))
                        pool.wait_ge(S["u_psum"][s], before(n))
                        pool.tensor_tensor(rhs[s][:], vn[s][:], ksg[s][0:R, :, :], ALU.subtract).then_inc(S["rhs_done"][s], 1)
                    for s in range(2):
                        pool.wait_ge(S["fac_done"][s], now(n))
                        pool.wait_ge(S["og_done"][s], before(n))
                        pool.tensor_tensor(otf[s][:], ot[s][:], fac[s][:], ALU.mult).then_inc(S["otf_done"][s], 1)
                    for s in range(2):
                        pool.wait_ge(S["otf_done"][s], now(n))
                        pool.wait_ge(seq["wo_psum"], before(b))
                        pool.wait_ge(seq["gatew_done"], now(b))
                        pool.tensor_tensor(og[:, s * GH:(s + 1) * GH, bass.ds(c * C, C)], otf[s][:],
                                           gate[:, s * GH:(s + 1) * GH, bass.ds(c * C, C)], ALU.mult).then_inc(S["og_done"][s], 1)

        @block.scalar
        def _(act):
            act.wait_ge(weights_in, 128)
            act.wait_ge(const_done, 1)
            act.activation(expa[:], alog[:], ACT.Exp).then_inc(expa_done, 1)
            with act.Fori(0, NB) as b:
                for i in range((NCONV + H) // 2):
                    act.wait_ge(seq["proj"], now(b, i + 1, (NCONV + H) // 2))
                    if 2 * i < NCONV:
                        if i == 0:
                            for s in range(2):
                                act.wait_ge(S["v_done"][s], before(b, NC))
                        for k in range(2):
                            ins = act.activation(y[:, 2 * i + k, :], bank[i % 8][:, k * T:(k + 1) * T], ACT.Copy, scale=cw[:, 2 * i + k, TAPS - 1:TAPS])
                        ins.then_inc(seq["tap0"], 1)
                    else:
                        if 2 * i == NCONV:
                            for s in range(2):
                                act.wait_ge(S["og_done"][s], before(b, NC))
                        act.activation(gate[:, 2 * i - NCONV:2 * i - NCONV + 2, :], bank[i % 8][:].rearrange("p (k t) -> p k t", k=2), ACT.Silu).then_inc(seq["gate_done"], 1)
                for i in range(NCONV // H):
                    act.wait_ge(seq["taps_done"], now(b, (i + 1) * H // 2, NCONV // 2))
                    act.activation(y[:, i * H:(i + 1) * H, :], y[:, i * H:(i + 1) * H, :], ACT.Silu).then_inc(seq["silu_done"], 1)
                act.wait_ge(seq["gate_done"], now(b, H // 2, H // 2))
                act.activation(gate[:], gate[:], ACT.Copy, scale=rmsw[:, 0:1]).then_inc(seq["gatew_done"], 1)
                act.wait_ge(seq["bg_psum"], now(b))
                act.activation(beta_t[:], bank[0][0:R, 0:NC * NK].rearrange("p (c i h) -> p c i h", c=NC, i=NH), ACT.Tanh, scale=0.5).then_inc(seq["tanh_done"], 1)
                act.wait_ge(seq["abs_done"], now(b))
                act.activation(ez[:], az[:], ACT.Exp, scale=-1.0).then_inc(seq["exp_z"], 1)
                act.wait_ge(seq["decay_psum"], now(b))
                for s in range(2):
                    act.wait_ge(S["kd_done"][s], before(b, NC))
                    act.wait_ge(S["ksg_done"][s], before(b, NC))
                    act.wait_ge(S["dec_done"][s], before(b, NC))
                act.activation(decays[:], bank[2][:, 0:3 * NC * H].rearrange("p (k c h) -> p k c h", k=3, c=NC), ACT.Exp).then_inc(seq["decay_done"], 1)
                act.preload_act_table_set("natural_log_exp_and_others")
                with act.Fori(0, NC) as c:
                    n = b * NC + c
                    t0 = act.snap(c * C)
                    for s in range(2):
                        hs = s * GH
                        act.wait_ge(S["ks_psum"][s], before(n))
                        act.wait_ge(S["kt_psum"][s], before(n))
                        act.sem_inc(carrier, 1)
                        for i in range(NH):
                            act.activation(kq[s][:, :, 0:R].rearrange("p h (t i) -> p h t i", i=NH)[:, :, :, i],
                                           y[:, NQ + i * H + hs:NQ + i * H + hs + GH, bass.ds(t0, C)], ACT.Copy)
                        act.activation(kq[s][:, :, R:P], y[:, hs:hs + GH, bass.ds(t0, C)], ACT.Copy).then_inc(S["kq_done"][s], 1)
                        act.wait_ge(S["kq_done"][s], now(n))
                        act.wait_ge(S["rms_psum"][s], before(n))
                        act.activation(sq[s][:], kq[s][:], ACT.Square).then_inc(S["sq_done"][s], 1)
                    for s in range(2):
                        act.wait_ge(S["e_psum"][s], now(n))
                        act.activation(ex[s][:], bk[s][1][0:R, :].rearrange("p (h j) -> p h j", j=P), ACT.Exp).then_inc(S["ex_done"][s], 1)
                        act.wait_ge(S["ss_psum"][s], now(n))
                        act.activation(lnss[s][:], bk[s][2][0:R, 0:GH], ACT.Ln, bias=qeps[0:R, 0:1]).then_inc(S["ln_done"][s], 1)
                        act.wait_ge(S["ln_done"][s], now(n))
                        act.activation(vlen[s][:], lnss[s][:], ACT.Exp, scale=0.5).then_inc(S["vlen_done"][s], 1)
                    for s in range(2):
                        act.wait_ge(S["vt_psum"][s], before(n))
                        act.sem_inc(carrier, 1)
                        for i in range(NH):
                            ins = act.activation(vt[s][:].rearrange("p h (t i) -> p h t i", i=NH)[:, :, :, i],
                                                 y[:, NQ + NK + i * H + s * GH:NQ + NK + i * H + s * GH + GH, bass.ds(t0, C)], ACT.Copy)
                        ins.then_inc(S["v_done"][s], 1)
                    for l in range(LEVELS):
                        for s in range(2):
                            act.wait_ge(S["t_psum"][s], now(n, l + 1, LEVELS))
                            act.activation(MT[s][:], bk[s][3][0:R, 0:GH * R].rearrange("p (h j) -> p h j", j=R), ACT.Copy).then_inc(S["t_done"][s], 1)
                    for s in range(2):
                        act.wait_ge(S["u_psum"][s], now(n))
                        act.activation(w[s][:], bk[s][1][0:R, :].rearrange("p (h j) -> p h j", j=DV), ACT.Copy).then_inc(S["w_done"][s], 1)
                    for s in range(2):
                        act.wait_ge(S["o_psum"][s], now(n))
                        act.wait_ge(S["otf_done"][s], before(n))
                        act.activation(ot[s][:], bk[s][3][:, 0:P].rearrange("p (h j) -> p h j", j=C), ACT.Copy).then_inc(S["o_done"][s], 1)
                        act.wait_ge(S["o_done"][s], now(n))
                        act.activation(osq[s][:], ot[s][:], ACT.Square).then_inc(S["osq_done"][s], 1)
                    for s in range(2):
                        act.wait_ge(S["rms_psum"][s], now(n))
                        act.activation(lnf[s][:], bk[s][2][:, 0:P].rearrange("p (h j) -> p h j", j=C), ACT.Ln, bias=oeps[:, 0:1]).then_inc(S["lnf_done"][s], 1)
                    for s in range(2):
                        act.wait_ge(S["lnf_done"][s], now(n))
                        act.activation(fac[s][:], lnf[s][:], ACT.Exp, scale=-0.5).then_inc(S["fac_done"][s], 1)

        @block.vector
        def _(dve):
            dve.wait_ge(weights_in, 128)
            dve.wait_ge(const_done, 1)
            NP2 = NCONV // 2
            with dve.Fori(0, NB) as b:
                dve.wait_ge(seq["xb_loaded"], now(b, 16, 16))
                dve.wait_ge(seq["bg_psum"], before(b))
                dve.tensor_copy(xb3[:], xb[:].unsqueeze(2).broadcast_to([P, T, NH])).then_inc(seq["xb3_done"], 1)
                for i in range(NP2):
                    dve.wait_ge(seq["tap0"], now(b, i + 1, NP2))
                    for shift in range(1, TAPS):
                        for k in range(2):
                            blk = 2 * i + k
                            if shift > 1:
                                dve.wait_ge(seq["tap_step"], now(b, i * 2 * (TAPS - 2) + (shift - 2) * 2 + k + 1, NP2 * 2 * (TAPS - 2)))
                            ins = dve.scalar_tensor_tensor(
                                out=y[:, blk, shift:T], in0=bank[i % 8][:, k * T:k * T + T - shift],
                                scalar=cw[:, blk, TAPS - 1 - shift:TAPS - shift], in1=y[:, blk, shift:T], op0=ALU.mult, op1=ALU.add)
                            if shift < TAPS - 1:
                                ins.then_inc(seq["tap_step"], 1)
                    ins.then_inc(seq["taps_done"], 1)
                dve.wait_ge(seq["tanh_done"], now(b))
                dve.tensor_scalar(beta_t[:], beta_t[:], 1.0, None, ALU.add).then_inc(seq["beta1_done"], 1)
                dve.wait_ge(seq["beta1_done"], now(b))
                dve.tensor_tensor(beta_s[:], beta_t[:], ranksel[:].unsqueeze(1).unsqueeze(3).broadcast_to([R, NC, NH, H]), ALU.mult).then_inc(seq["betas_done"], 1)
                dve.wait_ge(seq["betas_done"], now(b))
                dve.tensor_reduce(beta[:], beta_s[:].rearrange("p c i h -> p c h i"), AX.X, ALU.add).then_inc(seq["beta_done"], 1)
                dve.wait_ge(seq["bg_psum"], now(b))
                dve.tensor_tensor(z[:], bank[1][0:C, 0:NC * H].rearrange("p (c h) -> p c h", c=NC), dtb[:].unsqueeze(1).broadcast_to([C, NC, H]), ALU.add).then_inc(seq["z_done"], 1)
                dve.wait_ge(seq["z_done"], now(b))
                dve.tensor_scalar(zp[:], z[:], 0.0, None, ALU.max)
                dve.scalar_tensor_tensor(out=az[:], in0=z[:], scalar=-1.0, in1=z[:], op0=ALU.mult, op1=ALU.max).then_inc(seq["abs_done"], 1)
                dve.wait_ge(seq["exp_z"], now(b))
                dve.tensor_scalar(ez2[:], ez[:], 2.0, None, ALU.add).then_inc(seq["plus2"], 1)
                dve.wait_ge(seq["plus2"], now(b))
                dve.reciprocal(ezr[:], ez2[:]).then_inc(seq["recip_z"], 1)
                dve.wait_ge(seq["recip_z"], now(b))
                dve.tensor_tensor(sz[:], ez[:], ezr[:], ALU.mult).then_inc(seq["s_done"], 1)
                dve.wait_ge(seq["s_done"], now(b))
                dve.tensor_tensor(sz2[:], sz[:], sz[:], ALU.mult).then_inc(seq["s2_done"], 1)
                dve.wait_ge(seq["s2_done"], now(b))
                NS = len(ATANH) - 1
                dve.tensor_scalar(poly[:], sz2[:], ATANH[NS], ATANH[NS - 1], ALU.mult, ALU.add).then_inc(seq["horner"], 1)
                steps = 1
                for j in range(NS - 2, -1, -1):
                    dve.wait_ge(seq["horner"], now(b, steps, 2 * NS - 1))
                    dve.tensor_tensor(poly[:], poly[:], sz2[:], ALU.mult).then_inc(seq["horner"], 1)
                    dve.wait_ge(seq["horner"], now(b, steps + 1, 2 * NS - 1))
                    dve.tensor_scalar(poly[:], poly[:], ATANH[j], None, ALU.add).then_inc(seq["horner"], 1)
                    steps += 2
                dve.wait_ge(seq["horner"], now(b, 2 * NS - 1, 2 * NS - 1))
                dve.tensor_tensor(poly[:], poly[:], sz[:], ALU.mult).then_inc(seq["softplus"], 1)
                dve.wait_ge(seq["softplus"], now(b, 1, 2))
                dve.scalar_tensor_tensor(out=poly[:], in0=poly[:], scalar=2.0, in1=zp[:], op0=ALU.mult, op1=ALU.add).then_inc(seq["softplus"], 1)
                dve.wait_ge(seq["softplus"], now(b, 2, 2))
                dve.wait_ge(expa_done, 1)
                dve.tensor_tensor(poly[:], poly[:], expa[:].unsqueeze(1).broadcast_to([C, NC, H]), ALU.mult).then_inc(seq["decay_in"], 1)
                dve.wait_ge(seq["decay_in"], now(b))
                for s in range(2):
                    dve.wait_ge(S["gr_done"][s], before(b, NC))
                dve.tensor_scalar(g[:], poly[:], -1.0, -BIG, ALU.mult, ALU.max).then_inc(seq["g_done"], 1)
                with dve.Fori(0, NC) as c:
                    n = b * NC + c
                    for s in range(2):
                        dve.wait_ge(S["ln_done"][s], now(n))
                        dve.tensor_scalar(sse[s][:], bk[s][2][0:R, 0:GH], QEPS, None, ALU.add).then_inc(S["sse_done"][s], 1)
                        dve.wait_ge(S["sse_done"][s], now(n))
                        dve.reciprocal(inv[s][:], sse[s][:]).then_inc(S["inv_done"][s], 1)
                        dve.wait_ge(S["inv_done"][s], now(n))
                        dve.wait_ge(S["m0_done"][s], before(n))
                        dve.tensor_tensor(bp[s][:], inv[s][:], beta[:, bass.ds(c, 1), s * GH:(s + 1) * GH].rearrange("p a h -> p (a h)"), ALU.mult).then_inc(S["bp_done"][s], 1)
                    for s in range(2):
                        dve.wait_ge(S["gram"][s], now(n))
                        dve.wait_ge(S["ex_done"][s], now(n))
                        dve.wait_ge(S["o_psum"][s], before(n))
                        dve.tensor_tensor(at[s][:], bk[s][0][0:R, :].rearrange("p (h j) -> p h j", j=P), ex[s][:], ALU.mult).then_inc(S["at_done"][s], 1)
                    for s in range(2):
                        dve.wait_ge(S["kt_psum"][s], now(n))
                        dve.wait_ge(S["su_psum"][s], before(n))
                        dve.tensor_tensor(kd[s][:], bk[s][0][0:R, :].rearrange("p (h j) -> p h j", j=P),
                                          decays[0:R, 1, bass.ds(c, 1), s * GH:(s + 1) * GH].rearrange("p a h -> p (a h)").unsqueeze(2).broadcast_to([R, GH, P]),
                                          ALU.mult).then_inc(S["kd_done"][s], 1)
                        dve.wait_ge(S["vt_psum"][s], now(n))
                        dve.wait_ge(S["vlen_done"][s], now(n))
                        dve.wait_ge(S["rhs_done"][s], before(n))
                        dve.tensor_tensor(vn[s][:], bk[s][1][0:R, :].rearrange("p (h j) -> p h j", j=DV),
                                          vlen[s][:].unsqueeze(2).broadcast_to([R, GH, DV]), ALU.mult).then_inc(S["vn_done"][s], 1)
                        dve.wait_ge(S["ks_psum"][s], now(n))
                        dve.wait_ge(S["o_psum"][s], before(n))
                        dve.tensor_tensor(ksg[s][:], bk[s][0][:].rearrange("p (h j) -> p h j", j=DV),
                                          decays[:, 0, bass.ds(c, 1), s * GH:(s + 1) * GH].rearrange("p a h -> p (a h)").unsqueeze(2).broadcast_to([P, GH, DV]),
                                          ALU.mult).then_inc(S["ksg_done"][s], 1)
                    for l in range(LEVELS):
                        for s in range(2):
                            dve.wait_ge(S["p_psum"][s], now(n, l + 1, LEVELS))
                            mask = block_mask[:, l, 0:FH[l]].unsqueeze(1).broadcast_to([R, GH, FH[l]])
                            dve.tensor_tensor(pl[s][:, :, 0:FH[l]], bk[s][2][0:R, 0:GH * FH[l]].rearrange("p (h j) -> p h j", h=GH), mask, ALU.mult).then_inc(S["p_done"][s], 1)
                        for s in range(2):
                            dve.wait_ge(S["m_psum"][s], now(n, l + 1, LEVELS))
                            if l == 0:
                                dve.wait_ge(S["m0_done"][s], now(n))
                            else:
                                dve.wait_ge(S["m_done"][s], now(n, l, LEVELS))
                            new = bk[s][2][0:R, 256:256 + GH * FH[l]].rearrange("p (h j) -> p h j", h=GH)
                            dve.tensor_tensor(fh(M[s][:], l), fh(M[s][:], l), compact(new, l), ALU.add).then_inc(S["m_done"][s], 1)
                    for s in range(2):
                        dve.wait_ge(S["su_psum"][s], now(n))
                        dve.wait_ge(S["dec_done"][s], now(n))
                        dve.tensor_tensor(st[s][:], st_dec[s][:], bk[s][0][:].rearrange("p (h j) -> p h j", j=DV), ALU.add).then_inc(S["st_done"][s], 1)
                dve.wait_ge(seq["wo_psum"], now(b))
                dve.wait_ge(seq["x1_loaded"], now(b, 16, 16))
                dve.wait_ge(seq["x2_stored"], before(b, 16))
                dve.tensor_tensor(x2[:], x1[:], bank[0][:, 0:TT * D].rearrange("p (t d) -> p t d", d=D), ALU.add).then_inc(seq["x2_done"], 1)

        @block.tensor
        def _(pe):
            pe.wait_ge(weights_in, 128)
            pe.wait_ge(const_done, 1)
            NPB = (NCONV + H) // 2
            with pe.Fori(0, NB) as b:
                pe.wait_ge(seq["xb_loaded"], now(b, 16, 16))
                pe.wait_ge(seq["x2_done"], before(b))
                for s in range(2):
                    pe.wait_ge(S["st_done"][s], before(b, NC))
                    pe.wait_ge(S["fac_done"][s], before(b, NC))
                    pe.wait_ge(S["o_done"][s], before(b, NC))
                for i in range(NPB):
                    if 8 <= i:
                        j = i - 8
                        pe.wait_ge(seq["taps_done"], now(b, j + 1, NCONV // 2))
                    for k in range(2):
                        blk = 2 * i + k
                        ins = pe.matmul(bank[i % 8][:, k * T:(k + 1) * T], wp[:, blk * P:(blk + 1) * P], xb[:], start=True, stop=True)
                    ins.then_inc(seq["proj"], 1)
                pe.wait_ge(seq["taps_done"], now(b, NCONV // 2, NCONV // 2))
                pe.wait_ge(seq["gate_done"], now(b, H // 2, H // 2))
                pe.wait_ge(seq["xb3_done"], now(b))
                for c in range(NC):
                    pe.matmul(bank[0][0:R, c * NK:(c + 1) * NK], xb3[:, c * C:(c + 1) * C, :].rearrange("p t i -> p (t i)"), wb[:], start=True, stop=True)
                for c in range(NC):
                    ins = pe.matmul(bank[1][0:C, c * H:(c + 1) * H], xb[:, c * C:(c + 1) * C], wa[:], start=True, stop=True)
                ins.then_inc(seq["bg_psum"], 1)
                pe.wait_ge(seq["g_done"], now(b))
                gv = g[:].rearrange("p c h -> p (c h)")
                for k, lhs in enumerate((upto, later_only, ones)):
                    ins = pe.matmul(bank[2][:, k * NC * H:(k + 1) * NC * H], lhs[0:C, :], gv, start=True, stop=True)
                ins.then_inc(seq["decay_psum"], 1)
                pe.wait_ge(seq["silu_done"], now(b, NCONV // H, NCONV // H))
                pe.wait_ge(seq["decay_done"], now(b))
                pe.wait_ge(seq["tanh_done"], now(b))
                pe.sem_inc(carrier, 1)
                with pe.Fori(0, NC) as c:
                    n = b * NC + c
                    for s in range(2):
                        pe.wait_ge(S["kq_done"][s], now(n))
                        pe.wait_ge(S["st_done"][s], before(n))
                        for h in range(GH):
                            ins = pe.matmul(bk[s][0][0:R, h * P:(h + 1) * P], kq[s][:, h, 0:R], kq[s][:, h, :], start=True, stop=True)
                        ins.then_inc(S["gram"][s], 1)
                        pe.wait_ge(S["gr_done"][s], now(n))
                        pe.wait_ge(S["w_done"][s], before(n))
                        pe.matmul(bk[s][1][0:R, :], later[:], gr[s][:].rearrange("p h j -> p (h j)"), start=True, stop=True).then_inc(S["e_psum"][s], 1)
                        pe.wait_ge(S["sq_done"][s], now(n))
                        pe.wait_ge(S["lnf_done"][s], before(n))
                        for h in range(GH):
                            ins = pe.matmul(bk[s][2][0:R, h:h + 1], sq[s][:, h, 0:R], ones[:, 0:1], start=True, stop=True)
                        ins.then_inc(S["ss_psum"][s], 1)
                    for s in range(2):
                        pe.wait_ge(S["at_done"][s], now(n))
                        for h in range(GH):
                            ins = pe.transpose(bk[s][0][0:R, h * P:(h + 1) * P], kq[s][:, h, 0:R], ident[:])
                        ins.then_inc(S["kt_psum"][s], 1)
                        pe.wait_ge(S["ex_done"][s], now(n))
                        pe.wait_ge(S["v_done"][s], now(n))
                        for h in range(GH):
                            ins = pe.transpose(bk[s][1][0:R, h * P:(h + 1) * P], vt[s][:, h, :], ident[:])
                        ins.then_inc(S["vt_psum"][s], 1)
                        pe.wait_ge(S["kd_done"][s], now(n))
                        pe.wait_ge(seq["st_zero"], now(b, 2, 2))
                        for h in range(GH):
                            ins = pe.matmul(bk[s][0][:, h * P:(h + 1) * P], kq[s][:, h, :], st[s][:, h, :], start=True, stop=True)
                        ins.then_inc(S["ks_psum"][s], 1)
                    for l in range(LEVELS):
                        for s in range(2):
                            if l == 0:
                                pe.wait_ge(S["m0_done"][s], now(n))
                                pe.wait_ge(S["ln_done"][s], now(n))
                                pe.wait_ge(S["sse_done"][s], now(n))
                            else:
                                pe.wait_ge(S["m_done"][s], now(n, l, LEVELS))
                            Ml = fh(M[s][:], l)
                            for h in range(GH):
                                ins = pe.matmul(bk[s][2][0:R, h * FH[l]:(h + 1) * FH[l]], at[s][:, h, 0:R], Ml[:, h], start=True, stop=True)
                            ins.then_inc(S["p_psum"][s], 1)
                        for s in range(2):
                            pe.wait_ge(S["p_done"][s], now(n, l + 1, LEVELS))
                            if l > 0:
                                pe.wait_ge(S["t_done"][s], now(n, l, LEVELS))
                            for h in range(GH):
                                lhs = M[s][:, h, :] if l == 0 else MT[s][:, h, :]
                                ins = pe.matmul(bk[s][2][0:R, 256 + h * FH[l]:256 + (h + 1) * FH[l]], lhs, pl[s][:, h, 0:FH[l]], start=True, stop=True)
                            ins.then_inc(S["m_psum"][s], 1)
                        for s in range(2):
                            pe.wait_ge(S["m_done"][s], now(n, l + 1, LEVELS))
                            if l == 0:
                                pe.wait_ge(S["o_done"][s], before(n))
                            for h in range(GH):
                                ins = pe.transpose(bk[s][3][0:R, h * R:(h + 1) * R], M[s][:, h, :], ident[0:R, 0:R])
                            ins.then_inc(S["t_psum"][s], 1)
                    for s in range(2):
                        pe.wait_ge(S["rhs_done"][s], now(n))
                        pe.wait_ge(S["t_done"][s], now(n, LEVELS, LEVELS))
                        for h in range(GH):
                            ins = pe.matmul(bk[s][1][0:R, h * P:(h + 1) * P], MT[s][:, h, :], rhs[s][:, h, :], start=True, stop=True)
                        ins.then_inc(S["u_psum"][s], 1)
                    for s in range(2):
                        pe.wait_ge(S["w_done"][s], now(n))
                        pe.wait_ge(S["ksg_done"][s], now(n))
                        for h in range(GH):
                            ins = pe.matmul(bk[s][0][:, h * P:(h + 1) * P], kd[s][:, h, :], w[s][:, h, :], start=True, stop=True)
                        ins.then_inc(S["su_psum"][s], 1)
                        for h in range(GH):
                            out = bk[s][3][:, h * C:(h + 1) * C]
                            pe.matmul(out, w[s][:, h, :], at[s][:, h, R:P], start=True, stop=False)
                            ins = pe.matmul(out, ksg[s][:, h, :], ident[:, R:P], start=False, stop=True)
                        ins.then_inc(S["o_psum"][s], 1)
                    for s in range(2):
                        pe.wait_ge(S["osq_done"][s], now(n))
                        pe.matmul(bk[s][2][:, 0:P], mean_dv[:], osq[s][:].rearrange("p h j -> p (h j)"), start=True, stop=False)
                        pe.matmul(bk[s][2][:, 0:P].rearrange("p (h j) -> p h j", h=GH), mean_eps[:], sq[s][:, :, R:P], start=False, stop=True).then_inc(S["rms_psum"][s], 1)
                for s in range(2):
                    pe.wait_ge(S["og_done"][s], now(b, NC, NC))
                    pe.wait_ge(S["st_done"][s], now(b, NC, NC))
                for t in range(TT):
                    for h in range(H):
                        ins = pe.matmul(bank[0][:, t * D:(t + 1) * D], og[:, h, t * P:(t + 1) * P], wo[:, h, :], start=h == 0, stop=h == H - 1)
                ins.then_inc(seq["wo_psum"], 1)
    end_phase(nc, m)


def expert_layer(nc, x2_dram, xn2t_dram, router_t, w1_t, b1_t, w2_t, b2, out):
    E, F, TB = 8, 512, 512
    FB, NT = F // P, TB // P
    LOOPS = NTOK // TB
    with ExitStack() as ctx:
        m = Memory(nc, ctx, "moe")
        rw = m.sb("rw", [P, E])
        w1 = m.sb("w1", [P, E, F])
        b1 = m.sb("b1", [P, E, FB])
        w2 = m.sb("w2", [P, E, FB, D])
        b2s = m.sb("b2s", [E, D])
        ident = m.sb("ident", [P, P])
        expert_id = m.sb("expert_id", [P, E])
        xs = m.sb("xs", [P, 2, TB])
        x2 = m.sb("x2", [P, NT, D])
        top = m.sb("top", [P, NT, 8])
        topi = m.sb("topi", [P, NT, 8], u32)
        topf = m.sb("topf", [P, NT, 2])
        gap = m.sb("gap", [P, NT])
        egap = m.sb("egap", [P, NT])
        den = m.sb("den", [P, NT])
        wt = m.sb("wt", [P, 2, NT])
        first = m.sb("first", [P, NT, E])
        second = m.sb("second", [P, NT, E])
        gates = m.sb("gates", [P, NT, E])
        gatesT = m.sb("gatesT", [E, NT, P])
        h1 = m.sb("h1", [P, 2, FB, TB])
        acc = m.sb("acc", [P, NT, D])
        bank = m.banks(8)

        weights_in = m.sem("weights_in")
        const_step = m.sem("const_step")
        const_done = m.sem("const_done")
        UNPRIMED = len(m.semaphores)
        (x_loaded, x2_loaded, logits, top_done, topi_done, topf_done, gap_done, egap_done, den_done, wt0_done, wt_done,
         first_done, second_done, gates_done, gatesT_psum, gatesT_done, bias_psum, hidden, h1_done, expert_out, acc_done,
         stored) = [m.sem(k) for k in (
             "x_loaded x2_loaded logits top_done topi_done topf_done gap_done egap_done den_done wt0_done wt_done "
             "first_done second_done gates_done gatesT_psum gatesT_done bias_psum hidden h1_done expert_out acc_done stored").split()]
        carrier = m.sem("carrier")
        block = ctx.enter_context(nc.Block())

        @block.sync
        def _(sp):
            for s in m.semaphores[UNPRIMED:]:
                sp.sem_inc(s, 1)
            for dst, src in ((rw[:], router_t), (w1[:], w1_t), (b1[:], b1_t), (b2s[:], b2), (w2[:], w2_t)):
                sp.dma_start(dst, src).then_inc(weights_in, 16)
            with sp.Fori(0, LOOPS) as n:
                tok = sp.snap(n * TB)
                sp.wait_ge(hidden, before(n, E * FB))
                sp.sem_inc(carrier, 1)
                sp.dma_start(xs[:, 0, :], xn2t_dram[:, bass.ds(tok, TB)]).then_inc(x_loaded, 16)
                sp.wait_ge(acc_done, before(n, NT * (E + 1)))
                sp.sem_inc(carrier, 1)
                sp.dma_start(x2[:], x2_dram[bass.ds(tok, TB), :].rearrange("(t p) d -> p t d", p=P)).then_inc(x2_loaded, 16)
                sp.wait_ge(acc_done, now(n, NT * (E + 1), NT * (E + 1)))
                sp.sem_inc(carrier, 1)
                sp.dma_start(out[bass.ds(tok, TB), :].rearrange("(t p) d -> p t d", p=P), acc[:]).then_inc(stored, 16)
            sp.wait_ge(stored, 16 * LOOPS + 1)

        @block.gpsimd
        def _(pool):
            pool.memset(ident[:], 0.0).then_inc(const_step, 1)
            pool.wait_ge(const_step, 1)
            pool.affine_select(out=ident[:], in_=ident[:], compare_op=ALU.not_equal, fill=1.0, base=0,
                               pattern=[[-1, P]], channel_multiplier=1).then_inc(const_done, 1)
            for e in range(E):
                ins = pool.memset(expert_id[:, e:e + 1], float(e))
            ins.then_inc(const_done, 1)

        @block.scalar
        def _(act):
            act.wait_ge(weights_in, 80)
            with act.Fori(0, LOOPS) as n:
                act.wait_ge(gap_done, now(n))
                act.activation(egap[:], gap[:], ACT.Exp).then_inc(egap_done, 1)
                act.wait_ge(gatesT_psum, now(n))
                act.activation(gatesT[:], bank[7][0:E, :].rearrange("p (t q) -> p t q", q=P), ACT.Copy).then_inc(gatesT_done, 1)
                for e in range(E):
                    if e >= 2:
                        act.wait_ge(expert_out, now(n, e - 1, E))
                    else:
                        act.wait_ge(expert_out, before(n, E))
                    for f in range(FB):
                        act.wait_ge(hidden, now(n, e * FB + f + 1, E * FB))
                        act.activation(h1[:, e % 2, f, :], bank[f][:], ACT.Gelu, bias=b1[:, e, f:f + 1]).then_inc(h1_done, 1)

        @block.vector
        def _(dve):
            dve.wait_ge(const_done, 2)
            with dve.Fori(0, LOOPS) as n:
                dve.wait_ge(logits, now(n))
                dve.sem_inc(carrier, 1)
                for t in range(NT):
                    dve.max(top[:, t, :], bank[6][:, t * E:(t + 1) * E]).then_inc(top_done, 1)
                dve.wait_ge(top_done, now(n, NT, NT))
                dve.sem_inc(carrier, 1)
                for t in range(NT):
                    dve.max_index(topi[:, t, :], top[:, t, :], bank[6][:, t * E:(t + 1) * E]).then_inc(topi_done, 1)
                dve.tensor_tensor(gap[:], top[:, :, 1], top[:, :, 0], ALU.subtract).then_inc(gap_done, 1)
                dve.wait_ge(topi_done, now(n, NT, NT))
                dve.tensor_copy(topf[:], topi[:, :, 0:2]).then_inc(topf_done, 1)
                dve.wait_ge(egap_done, now(n))
                dve.tensor_scalar(den[:], egap[:], 1.0, None, ALU.add).then_inc(den_done, 1)
                dve.wait_ge(den_done, now(n))
                dve.reciprocal(wt[:, 0, :], den[:]).then_inc(wt0_done, 1)
                dve.wait_ge(wt0_done, now(n))
                dve.tensor_tensor(wt[:, 1, :], wt[:, 0, :], egap[:], ALU.mult).then_inc(wt_done, 1)
                dve.wait_ge(wt_done, now(n))
                dve.wait_ge(topf_done, now(n))
                for t in range(NT):
                    dve.tensor_scalar(first[:, t, :], expert_id[:], topf[:, t, 0:1], wt[:, 0, t:t + 1], ALU.is_equal, ALU.mult).then_inc(first_done, 1)
                    dve.tensor_scalar(second[:, t, :], expert_id[:], topf[:, t, 1:2], wt[:, 1, t:t + 1], ALU.is_equal, ALU.mult).then_inc(second_done, 1)
                dve.wait_ge(first_done, now(n, NT, NT))
                dve.wait_ge(second_done, now(n, NT, NT))
                dve.tensor_tensor(gates[:], first[:], second[:], ALU.add).then_inc(gates_done, 1)
                dve.wait_ge(bias_psum, now(n))
                dve.wait_ge(x2_loaded, now(n, 16, 16))
                dve.wait_ge(stored, before(n, 16))
                for t in range(NT):
                    dve.tensor_tensor(acc[:, t, :], x2[:, t, :], bank[7][:, t * P:(t + 1) * P], ALU.add).then_inc(acc_done, 1)
                for e in range(E):
                    dve.wait_ge(expert_out, now(n, e + 1, E))
                    for t in range(NT):
                        dve.wait_ge(acc_done, now(n, e * NT + t + 1, NT * (E + 1)))
                        dve.scalar_tensor_tensor(out=acc[:, t, :], in0=bank[4 + e % 2][:, t * D:(t + 1) * D], scalar=gates[:, t, e:e + 1],
                                                 in1=acc[:, t, :], op0=ALU.mult, op1=ALU.add).then_inc(acc_done, 1)

        @block.tensor
        def _(pe):
            pe.wait_ge(weights_in, 80)
            pe.wait_ge(const_done, 2)
            with pe.Fori(0, LOOPS) as n:
                pe.wait_ge(x_loaded, now(n, 16, 16))
                pe.wait_ge(topi_done, before(n, NT))
                for t in range(NT):
                    ins = pe.matmul(bank[6][:, t * E:(t + 1) * E], xs[:, 0, t * P:(t + 1) * P], rw[:], start=True, stop=True)
                ins.then_inc(logits, 1)

                def hidden_layer(e):
                    for f in range(FB):
                        if e == 0:
                            pe.wait_ge(h1_done, before(n, E * FB))
                        else:
                            pe.wait_ge(h1_done, now(n, (e - 1) * FB + f + 1, E * FB))
                        pe.matmul(bank[f][:], w1[:, e, f * P:(f + 1) * P], xs[:, 0, :], start=True, stop=True).then_inc(hidden, 1)

                def output_layer(e):
                    pe.wait_ge(h1_done, now(n, (e + 1) * FB, E * FB))
                    if e >= 2:
                        pe.wait_ge(acc_done, now(n, e * NT, NT * (E + 1)))
                    else:
                        pe.wait_ge(acc_done, before(n, NT * (E + 1)))
                    for t in range(NT):
                        for f in range(FB):
                            ins = pe.matmul(bank[4 + e % 2][:, t * D:(t + 1) * D], h1[:, e % 2, f, t * P:(t + 1) * P], w2[:, e, f, :],
                                            start=f == 0, stop=f == FB - 1)
                    ins.then_inc(expert_out, 1)

                hidden_layer(0)
                pe.wait_ge(gates_done, now(n))
                pe.wait_ge(acc_done, before(n, NT * (E + 1)))
                for t in range(NT):
                    ins = pe.transpose(bank[7][0:E, t * P:(t + 1) * P], gates[:, t, :], ident[:])
                ins.then_inc(gatesT_psum, 1)
                pe.wait_ge(gatesT_done, now(n))
                for t in range(NT):
                    ins = pe.matmul(bank[7][:, t * D:(t + 1) * D], gatesT[:, t, :], b2s[:], start=True, stop=True)
                ins.then_inc(bias_psum, 1)
                for e in range(E):
                    if e + 1 < E:
                        hidden_layer(e + 1)
                    output_layer(e)
    end_phase(nc, m)


def forward(nc, *, x, w_qkv, w_out, w_fp8_t, ffn_bias, in_scale, w_scale, w_proj, conv_w, w_beta, w_decay,
            a_log, dt_bias, rms_w, w_o, router_t, w1_t, b1_t, w2_t, b2, out):
    x1 = nc.dram_tensor("x1_dram", (NTOK, D), fp32, kind="Internal").ap()
    x2 = nc.dram_tensor("x2_dram", (NTOK, D), fp32, kind="Internal").ap()
    xn2t = nc.dram_tensor("xn2t_dram", (D, NTOK), fp32, kind="Internal").ap()
    local_attention_layer(nc, x, w_qkv, w_out, w_fp8_t, ffn_bias, in_scale, w_scale, x1, xn2t)
    delta_attention_layer(nc, x1, xn2t, w_proj, conv_w, w_beta, w_decay, a_log, dt_bias, rms_w, w_o, x2)
    expert_layer(nc, x2, xn2t, router_t, w1_t, b1_t, w2_t, b2, out)


def kernel(**inputs):
    import numpy as _np
    import concourse.bacc as _bacc
    from concourse.bass_utils import run_bass_kernel_spmd as _run

    I = {k: _np.asarray(v) for k, v in inputs.items()}
    H, E = 8, 8
    channels = lambda a, n: a.reshape(n, P, -1).transpose(1, 0, 2)
    laid = {
        "x": I["L0_attn_x"].reshape(NTOK, D),
        "w_qkv": I["L0_attn_w_qkv"],
        "w_out": I["L0_attn_w_out"],
        "w_fp8_t": I["L0_ffn_weight_fp8"].T,
        "ffn_bias": I["L0_ffn_bias"].reshape(1, D),
        "in_scale": I["L0_ffn_input_scale"].reshape(1, 1),
        "w_scale": I["L0_ffn_weight_scale"].reshape(1, 1),
        "w_proj": _np.concatenate([I["L1_attn_" + k] for k in ("Wq", "Wk", "Wv", "Wg")], 1),
        "conv_w": channels(_np.concatenate([I["L1_attn_conv_" + k] for k in "qkv"], 0), 7 * H),
        "w_beta": I["L1_attn_Wb"],
        "w_decay": I["L1_attn_Wa"],
        "a_log": I["L1_attn_A_log"].reshape(1, H),
        "dt_bias": I["L1_attn_dt_bias"].reshape(1, H),
        "rms_w": I["L1_attn_rms_weight"].reshape(P, 1),
        "w_o": channels(I["L1_attn_Wo"], H),
        "router_t": I["L1_ffn_router_w"].T,
        "w1_t": I["L1_ffn_w1"].transpose(2, 0, 1),
        "b1_t": I["L1_ffn_b1"].reshape(E, -1, P).transpose(2, 0, 1),
        "w2_t": I["L1_ffn_w2"].reshape(E, D, -1, P).transpose(3, 0, 2, 1),
        "b2": I["L1_ffn_b2"],
    }
    nc = _bacc.Bacc("TRN2", target_bir_lowering=False, num_devices=1)
    arrays, args = {}, {}
    for name, a in laid.items():
        a = _np.ascontiguousarray(a)
        arrays[f"in_{name}"] = a
        args[name] = nc.dram_tensor(f"in_{name}", a.shape, mybir.dt.from_np(a.dtype), kind="ExternalInput").ap()
    args["out"] = nc.dram_tensor("out_0", (NTOK, D), fp32, kind="ExternalOutput").ap()
    forward(nc, **args)
    r = _run(nc, [arrays], core_ids=[0])
    return r.results[0]["out_0"].reshape(NB, T, D)
```

```python
import concourse.bass as bass
from concourse import mybir
from contextlib import ExitStack

fp32 = mybir.dt.float32
i32 = mybir.dt.int32
u32 = mybir.dt.uint32
ALU = mybir.AluOpType
ACT = mybir.ActivationFunctionType
AX = mybir.AxisListType

P = 128
NB, T, D = 16, 256, 128
NTOK = NB * T
TT = T // P
NEG = -1.0e30
EPS = 1e-5


def now(n, k=1, per=1):
    return n * per + (k + 1)


def before(n, per=1):
    return n * per + 1


class Memory:

    def __init__(self, nc, ctx, phase):
        self.nc, self.ctx, self.phase, self.semaphores = nc, ctx, phase, []

    def sb(self, name, shape, dt=fp32):
        return self.ctx.enter_context(self.nc.sbuf_tensor(f"{self.phase}_{name}", shape, dt))

    def banks(self, count):
        return [self.ctx.enter_context(self.nc.psum_tensor(f"{self.phase}_bank{i}", [P, 512], fp32))
                for i in range(count)]

    def sem(self, name):
        s = self.nc.alloc_semaphore(f"{self.phase}_{name}")
        self.semaphores.append(s)
        return s

    def pair(self, name):
        return [self.sem(f"{name}{s}") for s in range(2)]


def end_phase(nc, m):
    nc.clear_and_free_semaphores(m.semaphores)
    nc.all_engine_barrier()


def local_attention_layer(nc, x, w_qkv, w_out, w_fp8_t, ffn_bias, in_scale, w_scale, x1_dram, xn2t_dram):
    H, HD, W = 16, 8, 64
    CAP = 448.0
    ROUNDS = [(0, 4 * r, 4, P) for r in range(4)] + [(1, 2 * r, 2, 3 * W) for r in range(8)]
    NR = len(ROUNDS)
    with ExitStack() as ctx:
        m = Memory(nc, ctx, "l0")
        wqkv = m.sb("wqkv", [P, 3 * D])
        wout = m.sb("wout", [P, D])
        w8 = m.sb("w8", [P, D])
        wdq = m.sb("wdq", [P, D])
        biasrow = m.sb("biasrow", [1, D])
        ones = m.sb("ones", [1, P])
        ident = m.sb("ident", [P, P])
        mask0 = m.sb("mask0", [P, P])
        mask1 = m.sb("mask1", [P, 3 * W])
        headmask = m.sb("headmask", [P, H])
        eps = m.sb("eps", [P, 1])
        s_in = m.sb("s_in", [P, 1])
        s_inv = m.sb("s_inv", [P, 1])
        s_w = m.sb("s_w", [P, 1])

        def two(name, shape, dt=fp32):
            return [m.sb(f"{name}{s}", shape, dt) for s in range(2)]

        xin = two("xin", [P, TT, D])
        stats = two("stats", [P, TT, 6])
        mv = two("mv", [P, TT, 2])
        lnv = two("lnv", [P, TT])
        rstd0 = two("rstd0", [P, TT])
        rr = two("rr", [P, TT])
        rv = two("rv", [P, TT])
        rstd = two("rstd", [P, TT])
        xnq = two("xnq", [P, 2 * TT, D])
        ebits = two("ebits", [P, TT, D])
        xT = two("xT", [P, 2 * TT, P])
        qT = two("qT", [P, T])
        kT = two("kT", [P, T])
        kTm = two("kTm", [P, H, T])
        vaug = two("vaug", [P, 3, H, HD + 1])
        mx = two("mx", [P, 2, 4])
        pr = two("pr", [P, 2, 512])
        pT = two("pT", [P, 2, 512])
        rden = two("rden", [P, TT, H])
        attn = two("attn", [P, TT, D])
        attnT = two("attnT", [P, TT, P])
        x1 = two("x1", [P, TT, D])
        xn2 = two("xn2", [P, TT, D])
        xn2T = two("xn2T", [P, T])
        bank = m.banks(8)
        bk = [bank[0:4], bank[4:8]]

        weights_in = m.sem("weights_in")
        const_step = m.sem("const_step")
        const_done = m.sem("const_done")
        wdq_done = m.sem("wdq_done")
        names = ("x_loaded x_norm_read stats_done var_done ln_done rstd0_done sq_done sv_done half_done rstd_done "
                 "xn_done xs_done xc_done eb_done magic_done up_done down_done xq_done "
                 "xT_psum xT_done qk_psum v_psum qT_done kT_done v_done kTm_done "
                 "scores max_done shifted probs probsT pT_done av_done rden_done attn_done "
                 "attnT_psum attnT_done out_psum x1_done xn2_done xn2T_psum xn2T_done").split()
        S = {k: m.pair(k) for k in names}
        x1_stored = m.pair("x1_stored")
        xn2T_stored = m.pair("xn2T_stored")
        carrier = m.sem("carrier")
        LOOPS = NB // 2
        block = ctx.enter_context(nc.Block())

        @block.sync
        def _(sp):
            for s in m.semaphores[4:]:
                sp.sem_inc(s, 1)
            with nc.allow_non_contiguous_dma(reason="small broadcasts"):
                sp.dma_start(wqkv[:], w_qkv).then_inc(weights_in, 16)
                sp.dma_start(wout[:], w_out).then_inc(weights_in, 16)
                sp.dma_start(w8[:], w_fp8_t).then_inc(weights_in, 16)
                sp.dma_start(biasrow[:], ffn_bias).then_inc(weights_in, 16)
                sp.dma_start(s_in[:], in_scale.broadcast_to([P, 1])).then_inc(weights_in, 16)
                sp.dma_start(s_w[:], w_scale.broadcast_to([P, 1])).then_inc(weights_in, 16)
            with sp.Fori(0, LOOPS) as n:
                tok = [sp.snap((n * 2 + s) * T) for s in range(2)]
                for s in range(2):
                    sp.wait_ge(S["x1_done"][s], before(n, TT))
                    sp.sem_inc(carrier, 1)
                    sp.dma_start(xin[s][:], x[bass.ds(tok[s], T), :].rearrange("(t p) d -> p t d", p=P)).then_inc(S["x_loaded"][s], 16)
                for s in range(2):
                    sp.wait_ge(S["x1_done"][s], now(n, TT, TT))
                    sp.sem_inc(carrier, 1)
                    sp.dma_start(x1_dram[bass.ds(tok[s], T), :].rearrange("(t p) d -> p t d", p=P), x1[s][:]).then_inc(x1_stored[s], 16)
                    sp.wait_ge(S["xn2T_done"][s], now(n))
                    sp.sem_inc(carrier, 1)
                    sp.dma_start(xn2t_dram[:, bass.ds(tok[s], T)], xn2T[s][:]).then_inc(xn2T_stored[s], 16)
            for s in range(2):
                sp.wait_ge(x1_stored[s], 16 * LOOPS + 1)
                sp.wait_ge(xn2T_stored[s], 16 * LOOPS + 1)

        @block.gpsimd
        def _(pool):
            pool.memset(ident[:], 0.0).then_inc(const_step, 1)
            pool.memset(mask0[:], 0.0).then_inc(const_step, 1)
            pool.memset(mask1[:], 0.0).then_inc(const_step, 1)
            pool.memset(headmask[:], 1.0).then_inc(const_step, 1)
            pool.memset(eps[:], EPS).then_inc(const_done, 1)
            pool.memset(ones[:], 1.0).then_inc(const_done, 1)
            for s in range(2):
                pool.memset(vaug[s][:], 1.0).then_inc(const_done, 1)
            pool.wait_ge(const_step, 4)
            pool.affine_select(out=ident[:], in_=ident[:], compare_op=ALU.not_equal, fill=1.0, base=0,
                               pattern=[[-1, P]], channel_multiplier=1).then_inc(const_done, 1)
            pool.affine_select(out=mask0[:], in_=mask0[:], compare_op=ALU.is_ge, fill=NEG, base=0,
                               pattern=[[-1, P]], channel_multiplier=1).then_inc(const_done, 1)
            pool.affine_select(out=mask1[:], in_=mask1[:], compare_op=ALU.is_ge, fill=NEG, base=W,
                               pattern=[[-1, 3 * W]], channel_multiplier=1).then_inc(const_step, 1)
            pool.affine_select(out=headmask[:], in_=headmask[:], compare_op=ALU.is_ge, fill=0.0, base=0,
                               pattern=[[-HD, H]], channel_multiplier=1).then_inc(const_step, 1)
            pool.wait_ge(const_step, 6)
            pool.memset(mask1[W:P, 0:W], NEG).then_inc(const_step, 1)
            pool.wait_ge(const_step, 7)
            pool.affine_select(out=headmask[:], in_=headmask[:], compare_op=ALU.is_ge, fill=0.0, base=HD - 1,
                               pattern=[[HD, H]], channel_multiplier=-1).then_inc(const_done, 1)
        CONSTS = 7

        @block.scalar
        def _(act):
            def rsqrt_seed(s, n, k):
                act.wait_ge(S["var_done"][s], now(n, k, 2))
                if k == 2:
                    act.wait_ge(S["half_done"][s], now(n, 1, 2))
                act.activation(lnv[s][:], mv[s][:, :, 1], ACT.Ln, bias=eps[:, 0:1]).then_inc(S["ln_done"][s], 1)
                act.wait_ge(S["ln_done"][s], now(n, k, 2))
                act.activation(rstd0[s][:], lnv[s][:], ACT.Exp, scale=-0.5).then_inc(S["rstd0_done"][s], 1)

            act.wait_ge(const_done, CONSTS)
            act.preload_act_table_set("natural_log_exp_and_others")
            with act.Fori(0, LOOPS) as n:
                for s in range(2):
                    rsqrt_seed(s, n, 1)
                for s in range(2):
                    act.wait_ge(S["xT_psum"][s], now(n))
                    act.activation(xT[s][:], bk[s][0][:].rearrange("p (a b) -> p a b", b=P), ACT.Copy).then_inc(S["xT_done"][s], 1)
                for s in range(2):
                    act.wait_ge(S["qk_psum"][s], now(n))
                    act.wait_ge(S["scores"][s], before(n, NR))
                    act.activation(qT[s][:], bk[s][1][:, 0:T], ACT.Copy, scale=float(HD) ** -0.5).then_inc(S["qT_done"][s], 1)
                    act.wait_ge(S["kTm_done"][s], before(n))
                    act.activation(kT[s][:], bk[s][1][:, T:2 * T], ACT.Copy).then_inc(S["kT_done"][s], 1)
                    act.wait_ge(S["v_psum"][s], now(n))
                    act.wait_ge(S["av_done"][s], before(n, NR))
                    act.activation(vaug[s][:, 0:2, :, 0:HD],
                                   bk[s][2][:, 0:2 * D].rearrange("p (v h e) -> p v h e", v=2, e=HD), ACT.Copy).then_inc(S["v_done"][s], 1)
                    act.activation(vaug[s][0:W, 2, :, 0:HD],
                                   bk[s][2][0:W, 2 * D:3 * D].rearrange("p (h e) -> p h e", e=HD), ACT.Copy).then_inc(S["v_done"][s], 1)

                def probabilities(s, r):
                    w, h0, hb, nk = ROUNDS[r]
                    act.wait_ge(S["shifted"][s], now(n, r + 1, NR))
                    act.activation(pr[s][:, r % 2, 0:hb * nk], pr[s][:, r % 2, 0:hb * nk], ACT.Exp).then_inc(S["probs"][s], 1)

                def probabilities_T(s, r):
                    w, h0, hb, nk = ROUNDS[r]
                    act.wait_ge(S["probsT"][s], now(n, r + 1, NR))
                    if r >= 2:
                        act.wait_ge(S["av_done"][s], now(n, r - 1, NR))
                    if w == 0:
                        act.activation(pT[s][:, r % 2, :], bk[s][2][:], ACT.Copy).then_inc(S["pT_done"][s], 2)
                    else:
                        act.activation(pT[s][:, r % 2, 0:2 * P], bk[s][2][:, 0:2 * P], ACT.Copy).then_inc(S["pT_done"][s], 1)
                        act.activation(pT[s][0:W, r % 2, 2 * P:4 * P], bk[s][2][0:W, 2 * P:4 * P], ACT.Copy).then_inc(S["pT_done"][s], 1)

                for s in range(2):
                    probabilities(s, 0)
                for r in range(NR):
                    for s in range(2):
                        if r + 1 < NR:
                            probabilities(s, r + 1)
                        probabilities_T(s, r)
                for s in range(2):
                    act.wait_ge(S["attnT_psum"][s], now(n))
                    act.activation(attnT[s][:], bk[s][0][:, 0:T].rearrange("p (a b) -> p a b", b=P), ACT.Copy).then_inc(S["attnT_done"][s], 1)
                for s in range(2):
                    rsqrt_seed(s, n, 2)
                for s in range(2):
                    act.wait_ge(S["xn2T_psum"][s], now(n))
                    act.wait_ge(xn2T_stored[s], before(n, 16))
                    act.activation(xn2T[s][:], bk[s][2][:, 0:T], ACT.Copy).then_inc(S["xn2T_done"][s], 1)

        @block.vector
        def _(dve):
            dve.wait_ge(weights_in, 96)
            dve.reciprocal(s_inv[:], s_in[:]).then_inc(wdq_done, 1)
            dve.tensor_scalar(wdq[:], w8[:], s_w[:, 0:1], None, ALU.mult).then_inc(wdq_done, 1)
            dve.wait_ge(const_done, CONSTS)
            dve.wait_ge(wdq_done, 2)

            def moments(s, n, src, k):
                if k == 2:
                    dve.wait_ge(S["xn_done"][s], now(n, TT, TT))
                for t in range(TT):
                    dve.bn_stats(stats[s][:, t, :], src[s][:, t, :]).then_inc(S["stats_done"][s], 1)
                dve.wait_ge(S["stats_done"][s], now(n, TT * k, 2 * TT))
                dve.sem_inc(carrier, 1)
                for t in range(TT):
                    ins = dve.bn_aggr(mv[s][:, t, :], stats[s][:, t, :])
                ins.then_inc(S["var_done"][s], 1)

            def sharpen(s, n, k):
                dve.wait_ge(S["rstd0_done"][s], now(n, k, 2))
                dve.tensor_tensor(rr[s][:], rstd0[s][:], rstd0[s][:], ALU.mult).then_inc(S["sq_done"][s], 1)
                dve.wait_ge(S["sq_done"][s], now(n, k, 2))
                dve.scalar_tensor_tensor(out=rv[s][:], in0=mv[s][:, :, 1], scalar=eps[:, 0:1], in1=rr[s][:],
                                         op0=ALU.add, op1=ALU.mult).then_inc(S["sv_done"][s], 1)
                dve.wait_ge(S["sv_done"][s], now(n, k, 2))
                dve.tensor_scalar(rr[s][:], rv[s][:], -0.5, 1.5, ALU.mult, ALU.add).then_inc(S["half_done"][s], 1)
                dve.wait_ge(S["half_done"][s], now(n, k, 2))
                dve.tensor_tensor(rstd[s][:], rstd0[s][:], rr[s][:], ALU.mult).then_inc(S["rstd_done"][s], 1)
                dve.wait_ge(S["rstd_done"][s], now(n, k, 2))

            with dve.Fori(0, LOOPS) as n:
                for s in range(2):
                    dve.wait_ge(S["x_loaded"][s], now(n, 16, 16))
                    moments(s, n, xin, 1)
                for s in range(2):
                    sharpen(s, n, 1)
                    dve.wait_ge(S["xT_psum"][s], before(n))
                    for t in range(TT):
                        dve.tensor_scalar(xnq[s][:, t, :], xin[s][:, t, :], mv[s][:, t, 0:1], rstd[s][:, t:t + 1],
                                          ALU.subtract, ALU.mult).then_inc(S["xn_done"][s], 1)
                for s in range(2):
                    q = xnq[s][:, TT:2 * TT, :]
                    dve.wait_ge(S["xn_done"][s], now(n, TT, TT))
                    dve.tensor_scalar(q, xnq[s][:, 0:TT, :], s_inv[:, 0:1], CAP, ALU.mult, ALU.min).then_inc(S["xs_done"][s], 1)
                for s in range(2):
                    q = xnq[s][:, TT:2 * TT, :]
                    dve.wait_ge(S["xs_done"][s], now(n))
                    dve.tensor_scalar(q, q, -CAP, None, ALU.max).then_inc(S["xc_done"][s], 1)
                for s in range(2):
                    q = xnq[s][:, TT:2 * TT, :]
                    dve.wait_ge(S["xc_done"][s], now(n))
                    dve.tensor_scalar(ebits[s][:].bitcast(i32), q.bitcast(i32), 0x7F800000, None, ALU.bitwise_and).then_inc(S["eb_done"][s], 1)
                for s in range(2):
                    dve.wait_ge(S["eb_done"][s], now(n))
                    dve.tensor_scalar(ebits[s][:], ebits[s][:], 2.0 ** -6, 1.5 * 2.0 ** 20, ALU.max, ALU.mult).then_inc(S["magic_done"][s], 1)
                for s in range(2):
                    q = xnq[s][:, TT:2 * TT, :]
                    dve.wait_ge(S["magic_done"][s], now(n))
                    dve.tensor_tensor(q, q, ebits[s][:], ALU.add).then_inc(S["up_done"][s], 1)
                for s in range(2):
                    q = xnq[s][:, TT:2 * TT, :]
                    dve.wait_ge(S["up_done"][s], now(n))
                    dve.tensor_tensor(q, q, ebits[s][:], ALU.subtract).then_inc(S["down_done"][s], 1)
                for s in range(2):
                    q = xnq[s][:, TT:2 * TT, :]
                    dve.wait_ge(S["down_done"][s], now(n))
                    dve.tensor_scalar(q, q, s_in[:, 0:1], None, ALU.mult).then_inc(S["xq_done"][s], 1)
                for s in range(2):
                    dve.wait_ge(S["kT_done"][s], now(n))
                    dve.wait_ge(S["scores"][s], before(n, NR))
                    for h in range(H):
                        ins = dve.tensor_scalar(kTm[s][:, h, :], kT[s][:], headmask[:, h:h + 1], None, ALU.mult)
                    ins.then_inc(S["kTm_done"][s], 1)
                for r, (w, h0, hb, nk) in enumerate(ROUNDS):
                    for s in range(2):
                        sc = bk[s][r % 2][:, 0:hb * nk].rearrange("p (h k) -> p h k", k=nk)
                        dve.wait_ge(S["scores"][s], now(n, r + 1, NR))
                        dve.tensor_reduce(mx[s][:, r % 2, 0:hb], sc, AX.X, ALU.max).then_inc(S["max_done"][s], 1)
                    for s in range(2):
                        sc = bk[s][r % 2][:, 0:hb * nk].rearrange("p (h k) -> p h k", k=nk)
                        dve.wait_ge(S["max_done"][s], now(n, r + 1, NR))
                        if r >= 2:
                            dve.wait_ge(S["probsT"][s], now(n, r - 1, NR))
                        dve.tensor_tensor(pr[s][:, r % 2, 0:hb * nk].rearrange("p (h k) -> p h k", k=nk), sc,
                                          mx[s][:, r % 2, 0:hb].unsqueeze(2).broadcast_to([P, hb, nk]),
                                          ALU.subtract).then_inc(S["shifted"][s], 1)
                for s in range(2):
                    ao = bk[s][3][:, 0:TT * H * (HD + 1)].rearrange("p (w h e) -> p w h e", w=TT, e=HD + 1)
                    dve.wait_ge(S["av_done"][s], now(n, NR, NR))
                    dve.reciprocal(rden[s][:], ao[:, :, :, HD]).then_inc(S["rden_done"][s], 1)
                for s in range(2):
                    ao = bk[s][3][:, 0:TT * H * (HD + 1)].rearrange("p (w h e) -> p w h e", w=TT, e=HD + 1)
                    dve.wait_ge(S["rden_done"][s], now(n))
                    for w in range(TT):
                        dve.tensor_tensor(attn[s][:, w, :].rearrange("p (h e) -> p h e", e=HD), ao[:, w, :, 0:HD],
                                          rden[s][:, w, :].unsqueeze(2).broadcast_to([P, H, HD]), ALU.mult).then_inc(S["attn_done"][s], 1)
                for s in range(2):
                    dve.wait_ge(S["out_psum"][s], now(n))
                    dve.wait_ge(x1_stored[s], before(n, 16))
                    for t in range(TT):
                        dve.tensor_tensor(x1[s][:, t, :], xin[s][:, t, :], bk[s][1][:, t * D:(t + 1) * D], ALU.add).then_inc(S["x1_done"][s], 1)
                for s in range(2):
                    dve.wait_ge(S["x1_done"][s], now(n, TT, TT))
                    moments(s, n, x1, 2)
                for s in range(2):
                    sharpen(s, n, 2)
                    for t in range(TT):
                        dve.tensor_scalar(xn2[s][:, t, :], x1[s][:, t, :], mv[s][:, t, 0:1], rstd[s][:, t:t + 1],
                                          ALU.subtract, ALU.mult).then_inc(S["xn2_done"][s], 1)

        @block.tensor
        def _(pe):
            pe.wait_ge(weights_in, 96)
            pe.wait_ge(const_done, CONSTS)
            pe.wait_ge(wdq_done, 2)
            with pe.Fori(0, LOOPS) as n:
                for s in range(2):
                    pe.wait_ge(S["xq_done"][s], now(n))
                    for t in range(2 * TT):
                        ins = pe.transpose(bk[s][0][:, t * P:(t + 1) * P], xnq[s][:, t, :], ident[:])
                    ins.then_inc(S["xT_psum"][s], 1)
                for s in range(2):
                    xnT = xT[s][:, 0:TT, :].rearrange("p t q -> p (t q)")
                    pe.wait_ge(S["xT_done"][s], now(n))
                    pe.matmul(bk[s][1][:, 0:T], wqkv[:, 0:D], xnT, start=True, stop=True)
                    pe.matmul(bk[s][1][:, T:2 * T], wqkv[:, D:2 * D], xnT, start=True, stop=True).then_inc(S["qk_psum"][s], 1)
                    pe.wait_ge(S["xn2T_done"][s], before(n))
                    for v, (k0, rows) in enumerate(((0, P), (W, P), (3 * W, W))):
                        ins = pe.matmul(bk[s][2][0:rows, v * D:(v + 1) * D], xnT[:, k0:k0 + rows], wqkv[:, 2 * D:3 * D],
                                        start=True, stop=True)
                    ins.then_inc(S["v_psum"][s], 1)

                def scores(s, r):
                    w, h0, hb, nk = ROUNDS[r]
                    k0 = w * W
                    out = bk[s][r % 2][:, 0:hb * nk].rearrange("p (h k) -> p h k", k=nk)
                    if r == 0:
                        pe.wait_ge(S["qT_done"][s], now(n))
                        pe.wait_ge(S["kTm_done"][s], now(n))
                    if r >= 2:
                        pe.wait_ge(S["shifted"][s], now(n, r - 1, NR))
                    pe.matmul(out, qT[s][:, w * P:(w + 1) * P], kTm[s][:, h0:h0 + hb, k0:k0 + nk], start=True, stop=False)
                    mask = (mask0 if w == 0 else mask1)[:].unsqueeze(1).broadcast_to([P, hb, nk])
                    pe.matmul(out, ident[:], mask, start=False, stop=True).then_inc(S["scores"][s], 1)

                def transposes(s, r):
                    w, h0, hb, nk = ROUNDS[r]
                    pe.wait_ge(S["probs"][s], now(n, r + 1, NR))
                    if r == 0:
                        pe.wait_ge(S["v_done"][s], now(n, 2, 2))
                    else:
                        pe.wait_ge(S["pT_done"][s], now(n, 2 * r, 2 * NR))
                    for h in range(hb):
                        ins = pe.transpose(bk[s][2][:, h * P:(h + 1) * P], pr[s][:, r % 2, h * nk:h * nk + P], ident[:])
                    if w == 1:
                        for h in range(hb):
                            ins = pe.transpose(bk[s][2][0:W, (2 + h) * P:(3 + h) * P], pr[s][:, r % 2, h * nk + P:(h + 1) * nk], ident[:])
                    ins.then_inc(S["probsT"][s], 1)

                def values(s, r):
                    w, h0, hb, nk = ROUNDS[r]
                    pe.wait_ge(S["pT_done"][s], now(n, 2 * r + 2, 2 * NR))
                    if r == 0:
                        pe.wait_ge(S["attn_done"][s], before(n, TT))
                    for h in range(hb):
                        c = (w * H + h0 + h) * (HD + 1)
                        out = bk[s][3][:, c:c + HD + 1]
                        ins = pe.matmul(out, pT[s][:, r % 2, h * P:(h + 1) * P], vaug[s][:, w, h0 + h, :], start=True, stop=w == 0)
                        if w == 1:
                            ins = pe.matmul(out, pT[s][0:W, r % 2, (2 + h) * P:(3 + h) * P], vaug[s][0:W, 2, h0 + h, :], start=False, stop=True)
                    ins.then_inc(S["av_done"][s], 1)

                for r in range(NR + 1):
                    for s in range(2):
                        if r < NR:
                            scores(s, r)
                    for s in range(2):
                        if r >= 1:
                            transposes(s, r - 1)
                    for s in range(2):
                        if r >= 1:
                            values(s, r - 1)
                for s in range(2):
                    pe.wait_ge(S["attn_done"][s], now(n, TT, TT))
                    pe.wait_ge(S["shifted"][s], now(n, NR, NR))
                    for t in range(TT):
                        ins = pe.transpose(bk[s][0][:, t * P:(t + 1) * P], attn[s][:, t, :], ident[:])
                    ins.then_inc(S["attnT_psum"][s], 1)
                for s in range(2):
                    pe.wait_ge(S["attnT_done"][s], now(n))
                    for t in range(TT):
                        out = bk[s][1][:, t * D:(t + 1) * D]
                        pe.matmul(out, attnT[s][:, t, :], wout[:], start=True, stop=False)
                        pe.matmul(out, xT[s][:, TT + t, :], wdq[:], start=False, stop=False)
                        ins = pe.matmul(out, ones[:], biasrow[:], start=False, stop=True)
                    ins.then_inc(S["out_psum"][s], 1)
                for s in range(2):
                    pe.wait_ge(S["xn2_done"][s], now(n, TT, TT))
                    pe.wait_ge(S["pT_done"][s], now(n, 2 * NR, 2 * NR))
                    for t in range(TT):
                        ins = pe.transpose(bk[s][2][:, t * P:(t + 1) * P], xn2[s][:, t, :], ident[:])
                    ins.then_inc(S["xn2T_psum"][s], 1)
    end_phase(nc, m)


def delta_attention_layer(nc, x1_dram, xn2t_dram, w_proj, conv_w, w_beta, w_decay, a_log, dt_bias, rms_w, w_o, x2_dram):
    H, NH, C, GH, DV = 8, 3, 32, 4, 128
    R = NH * C
    NC = T // C
    BIG = 2.0 ** 14
    NQ, NK, NV = H, NH * H, NH * H
    NCONV = NQ + NK + NV
    TAPS = 4
    LEVELS = 5
    TRANSPOSES = LEVELS + 1
    HALF = R // 2
    XSTEPS = 5
    QEPS, OEPS = 1e-6, 1e-5
    ATANH = [1.0 / (2 * j + 1) for j in range(8)]
    with ExitStack() as ctx:
        m = Memory(nc, ctx, "l1")
        wp = m.sb("wp", [P, (NCONV + H) * P])
        wo = m.sb("wo", [P, H, D])
        wb = m.sb("wb", [P, NK])
        wa = m.sb("wa", [P, H])
        cw = m.sb("cw", [P, NCONV, TAPS])
        alog = m.sb("alog", [C, H])
        expa = m.sb("expa", [C, H])
        dtb = m.sb("dtb", [C, H])
        rmsw = m.sb("rmsw", [P, 1])
        ident = m.sb("ident", [P, P])
        ones = m.sb("ones", [P, P])
        mean_dv = m.sb("mean_dv", [P, P])
        mean_eps = m.sb("mean_eps", [P, P])
        qeps = m.sb("qeps", [P, 1])
        oeps = m.sb("oeps", [P, 1])
        ranksel = m.sb("ranksel", [R, NH])
        later = m.sb("later", [P, R])
        later_only = m.sb("later_only", [C, P])
        upto = m.sb("upto", [C, P])
        block_mask = m.sb("block_mask", [R, LEVELS, HALF])
        same_token = m.sb("same_token", [R, C])
        xb = m.sb("xb", [P, T])
        xb3 = m.sb("xb3", [P, T, NH])
        y = m.sb("y", [P, NCONV, T])
        gate = m.sb("gate", [P, H, T])
        og = m.sb("og", [P, H, T])
        x1 = m.sb("x1", [P, TT, D])
        x2 = m.sb("x2", [P, TT, D])
        beta_t = m.sb("beta_t", [R, NC, NH, H])
        beta_s = m.sb("beta_s", [R, NC, NH, H])
        beta = m.sb("beta", [R, NC, H])
        z = m.sb("z", [C, NC, H])
        az = m.sb("az", [C, NC, H])
        zp = m.sb("zp", [C, NC, H])
        ez = m.sb("ez", [C, NC, H])
        ez2 = m.sb("ez2", [C, NC, H])
        ezr = m.sb("ezr", [C, NC, H])
        sz = m.sb("sz", [C, NC, H])
        sz2 = m.sb("sz2", [C, NC, H])
        poly = m.sb("poly", [C, NC, H])
        g = m.sb("g", [C, NC, H])
        decays = m.sb("decays", [P, 3, NC, H])

        def two(name, shape):
            return [m.sb(f"{name}{s}", shape) for s in range(2)]

        kq = two("kq", [P, GH, P])
        vt = two("vt", [P, GH, R])
        sq = [two(f"sq{p}_", [P, GH, P]) for p in range(2)]
        gr = two("gr", [P, GH, P])
        ex = two("ex", [R, GH, P])
        at_full = [two(f"at{p}_", [P, GH, P]) for p in range(2)]
        lnss = two("lnss", [R, GH])
        vlen = two("vlen", [R, GH])
        sse = two("sse", [R, GH])
        inv = two("inv", [R, GH])
        bp = two("bp", [R, GH])
        M_full = two("M", [P, GH, R])
        MT_full = two("MT", [P, GH, R])
        pl_full = two("pl", [P, GH, R])
        own_full = two("own", [P, GH, R])
        x_first_full = two("x_first", [P, GH, NH])
        bax = two("bax", [R, GH, NH])
        x_next_full = two("x_next", [P, GH, NH])
        kd_full = [two(f"kd{p}_", [P, GH, P]) for p in range(2)]
        vn = two("vn", [R, GH, DV])
        ksg = two("ksg", [P, GH, DV])
        rhs_full = two("rhs", [P, GH, DV])
        w_full = two("w", [P, GH, DV])
        st = two("st", [P, GH, DV])
        st_dec = two("st_dec", [P, GH, DV])
        ot = two("ot", [P, GH, C])
        osq = two("osq", [P, GH, C])
        lnf = two("lnf", [P, GH, C])
        fac = two("fac", [P, GH, C])
        otf = two("otf", [P, GH, C])
        zero_filled = [*at_full[0], *at_full[1], *kd_full[0], *kd_full[1], *M_full, *MT_full, *pl_full, *own_full,
                       *x_first_full, *x_next_full, *rhs_full, *w_full]
        at, kd = ([[t[0:R] for t in pair] for pair in full] for full in (at_full, kd_full))
        M, MT, pl, own, x_first, x_next, rhs, w = ([t[0:R] for t in full] for full in (
            M_full, MT_full, pl_full, own_full, x_first_full, x_next_full, rhs_full, w_full))
        bank = m.banks(8)
        bk = [bank[0:4], bank[4:8]]

        weights_in = m.sem("weights_in")
        const_step = m.sem("const_step")
        const_done = m.sem("const_done")
        expa_done = m.sem("expa_done")
        gr_init = m.sem("gr_init")
        UNPRIMED = len(m.semaphores)
        seq = {k: m.sem(k) for k in ("xb_loaded xb3_done proj tap0 taps_done silu_done gate_done gatew_done "
                                     "bg_psum tanh_done beta1_done betas_done beta_done z_done abs_done exp_z plus2 recip_z s_done s2_done "
                                     "tap_step horner softplus decay_in g_done decay_psum decay_done "
                                     "wo_psum x1_loaded x2_done x2_stored st_zero").split()}
        S = {k: m.pair(k) for k in ("kq_done v_done sq_done gr_done gram e_psum ss_psum ex_done at_done ln_done vlen_done "
                                    "sse_done inv_done bp_done own_done ax_psum x_step m0_done p_psum p_done m_psum m_done t_psum t_done "
                                    "kt_psum kd_done vt_psum vn_done ks_psum ksg_done rhs_done u_psum w_done dec_done su_psum st_done "
                                    "o_psum o_done osq_done rms_psum lnf_done fac_done otf_done og_done").split()}
        carrier = m.sem("carrier")
        block = ctx.enter_context(nc.Block())

        def chunks(engine, b, turn):
            turn(b * NC, 0, 0, True, False)
            with engine.Fori(0, (NC - 2) // 2) as j:
                for k in range(2):
                    c = engine.snap(j * 2 + (k + 1))
                    turn(b * NC + c, c, (k + 1) % 2, False, False)
            turn(b * NC + (NC - 1), NC - 1, (NC - 1) % 2, False, True)

        def per_head(t, c, s):
            return t[:, bass.ds(c, 1), s * GH:(s + 1) * GH].rearrange("p a h -> p (a h)").unsqueeze(2)

        def fh(t, l):
            return t.rearrange("p h (b two m) -> p h b two m", two=2, m=NH << l)[:, :, :, 0, :]

        def compact(t, l):
            return t.rearrange("p h (b m) -> p h b m", m=NH << l)

        def same():
            return same_token[:].unsqueeze(1).unsqueeze(3).broadcast_to([R, GH, C, NH])

        @block.sync
        def _(sp):
            for s in m.semaphores[UNPRIMED:]:
                sp.sem_inc(s, 1)
            with nc.allow_non_contiguous_dma(reason="small broadcasts"):
                sp.dma_start(wp[:], w_proj).then_inc(weights_in, 16)
                sp.dma_start(cw[:], conv_w).then_inc(weights_in, 16)
                sp.dma_start(wo[:], w_o).then_inc(weights_in, 16)
                sp.dma_start(wb[:], w_beta).then_inc(weights_in, 16)
                sp.dma_start(wa[:], w_decay).then_inc(weights_in, 16)
                sp.dma_start(alog[:], a_log.broadcast_to([C, H])).then_inc(weights_in, 16)
                sp.dma_start(dtb[:], dt_bias.broadcast_to([C, H])).then_inc(weights_in, 16)
                sp.dma_start(rmsw[:], rms_w).then_inc(weights_in, 16)
            with sp.Fori(0, NB) as b:
                tok = sp.snap(b * T)
                sp.wait_ge(seq["bg_psum"], before(b))
                sp.sem_inc(carrier, 1)
                sp.dma_start(xb[:], xn2t_dram[:, bass.ds(tok, T)]).then_inc(seq["xb_loaded"], 16)
                sp.wait_ge(seq["x2_done"], before(b))
                sp.sem_inc(carrier, 1)
                sp.dma_start(x1[:], x1_dram[bass.ds(tok, T), :].rearrange("(t p) d -> p t d", p=P)).then_inc(seq["x1_loaded"], 16)
                sp.wait_ge(seq["x2_done"], now(b))
                sp.sem_inc(carrier, 1)
                sp.dma_start(x2_dram[bass.ds(tok, T), :].rearrange("(t p) d -> p t d", p=P), x2[:]).then_inc(seq["x2_stored"], 16)
            sp.wait_ge(seq["x2_stored"], 16 * NB + 1)

        @block.gpsimd
        def _(pool):
            step = [0]

            def const(ins):
                step[0] += 1
                ins.then_inc(const_step, 1)
                pool.wait_ge(const_step, step[0])

            def select(t, pattern, base, ch, op=ALU.is_ge, fill=0.0):
                const(pool.affine_select(out=t, in_=t, compare_op=op, fill=fill, base=base, pattern=pattern, channel_multiplier=ch))

            const(pool.memset(ones[:], 1.0))
            const(pool.memset(mean_dv[:], 1.0 / DV))
            const(pool.memset(mean_eps[:], OEPS * DV))
            const(pool.memset(qeps[:], QEPS))
            const(pool.memset(oeps[:], OEPS * DV * QEPS))
            const(pool.memset(ident[:], 0.0))
            select(ident[:], [[-1, P]], 0, 1, ALU.not_equal, 1.0)
            const(pool.memset(ranksel[:], 0.0))
            for t in range(C):
                select(ranksel[:], [[-1, NH]], -NH * t, 1, ALU.not_equal, 1.0)
            const(pool.memset(later[:], 0.0))
            select(later[:], [[-1, R]], -C, 1, ALU.not_equal, 1.0)
            const(pool.memset(later[0:C, :], 1.0))
            select(later[0:C, :].rearrange("p (t i) -> p t i", i=NH), [[-1, C], [0, NH]], -1, 1)
            const(pool.memset(later_only[:], 0.0))
            const(pool.tensor_copy(later_only[:, 0:R], later[0:C, :]))
            const(pool.memset(upto[:], 1.0))
            select(upto[:, 0:R].rearrange("p (t i) -> p t i", i=NH), [[1, C], [0, NH]], 0, -1)
            select(upto[:, R:P], [[1, C]], 0, -1)
            const(pool.memset(block_mask[:], -1.0))
            for l in range(LEVELS):
                w_ = NH << l
                bm = block_mask[:, l, :].rearrange("p (b m) -> p b m", m=w_)
                select(bm, [[-2 * w_, HALF // w_], [0, w_]], -w_, 1)
                select(bm, [[2 * w_, HALF // w_], [0, w_]], 2 * w_ - 1, -1)
            const(pool.memset(same_token[:], 1.0))
            select(same_token[:], [[-NH, C]], 0, 1)
            select(same_token[:], [[NH, C]], NH - 1, -1)
            for s in range(2):
                const(pool.memset(gr[s][:], -BIG))
                select(gr[s][:, :, 0:R], [[0, GH], [-1, R]], -C, 1)
                select(gr[s][:, :, R:P], [[0, GH], [-NH, C]], -C - NH, 1)
            for t in zero_filled:
                const(pool.memset(t[:], 0.0))
            pool.drain().then_inc(const_done, 1)

            with pool.Fori(0, NB) as b:
                for s in range(2):
                    pool.wait_ge(S["st_done"][s], before(b, NC))
                    pool.wait_ge(S["dec_done"][s], before(b, NC))
                    pool.sem_inc(carrier, 1)
                    pool.memset(st[s][:], 0.0).then_inc(seq["st_zero"], 1)
                pool.wait_ge(seq["decay_done"], now(b))
                pool.sem_inc(carrier, 1)

                def decays_in(n1, c1):
                    for s in range(2):
                        pool.wait_ge(S["e_psum"][s], before(n1))
                        pool.tensor_tensor(gr[s][0:C, :, :], upto[:].unsqueeze(1).broadcast_to([C, GH, P]),
                                           per_head(g, c1, s).broadcast_to([C, GH, P]), ALU.mult).then_inc(S["gr_done"][s], 1)

                def start_m(n1):
                    for s in range(2):
                        pool.wait_ge(S["x_step"][s], now(n1, XSTEPS, XSTEPS))
                        pool.wait_ge(S["t_psum"][s], before(n1, TRANSPOSES))
                        pool.tensor_tensor(M[s][:].rearrange("p h (t i) -> p h t i", i=NH), same(),
                                           x_next[s][:].unsqueeze(2).broadcast_to([R, GH, C, NH]), ALU.mult).then_inc(S["m0_done"][s], 1)

                def own_products(n1, parity):
                    for s in range(2):
                        pool.wait_ge(S["at_done"][s], now(n1))
                        pool.wait_ge(S["ax_psum"][s], before(n1, 2))
                        pool.tensor_tensor(own[s][:].rearrange("p h (t i) -> p h t i", i=NH),
                                           at[parity][s][:, :, 0:R].rearrange("p h (t i) -> p h t i", i=NH), same(), ALU.mult).then_inc(S["own_done"][s], 1)

                def gated_norm(n0, c0):
                    for s in range(2):
                        pool.wait_ge(S["fac_done"][s], now(n0))
                        pool.wait_ge(S["og_done"][s], before(n0))
                        pool.tensor_tensor(otf[s][:], ot[s][:], fac[s][:], ALU.mult).then_inc(S["otf_done"][s], 1)
                    for s in range(2):
                        pool.wait_ge(S["otf_done"][s], now(n0))
                        pool.wait_ge(seq["wo_psum"], before(b))
                        pool.wait_ge(seq["gatew_done"], now(b))
                        pool.tensor_tensor(og[:, s * GH:(s + 1) * GH, bass.ds(c0 * C, C)], otf[s][:],
                                           gate[:, s * GH:(s + 1) * GH, bass.ds(c0 * C, C)], ALU.mult).then_inc(S["og_done"][s], 1)

                def turn(n, c, parity, first, last):
                    if not last:
                        decays_in(n + 1, c + 1)
                    for s in range(2):
                        pool.wait_ge(S["ksg_done"][s], now(n))
                        pool.wait_ge(S["vn_done"][s], now(n))
                        pool.wait_ge(S["u_psum"][s], before(n))
                        pool.tensor_tensor(rhs[s][:], vn[s][:], ksg[s][0:R, :, :], ALU.subtract).then_inc(S["rhs_done"][s], 1)
                    if not first:
                        gated_norm(n - 1, c - 1)
                    for s in range(2):
                        pool.wait_ge(S["st_done"][s], before(n))
                        pool.tensor_tensor(st_dec[s][:], st[s][:], per_head(decays[:, 2], c, s).broadcast_to([P, GH, DV]),
                                           ALU.mult).then_inc(S["dec_done"][s], 1)
                    if last:
                        gated_norm(n, c)
                    else:
                        own_products(n + 1, 1 - parity)
                        start_m(n + 1)

                decays_in(b * NC, 0)
                own_products(b * NC, 0)
                start_m(b * NC)
                pool.wait_ge(seq["st_zero"], now(b, 2, 2))
                pool.sem_inc(carrier, 1)
                chunks(pool, b, turn)

        @block.scalar
        def _(act):
            act.wait_ge(weights_in, 128)
            act.wait_ge(const_done, 1)
            act.activation(expa[:], alog[:], ACT.Exp).then_inc(expa_done, 1)
            with act.Fori(0, NB) as b:
                for i in range((NCONV + H) // 2):
                    act.wait_ge(seq["proj"], now(b, i + 1, (NCONV + H) // 2))
                    if 2 * i < NCONV:
                        if i == 0:
                            for s in range(2):
                                act.wait_ge(S["v_done"][s], before(b, NC))
                        for k in range(2):
                            ins = act.activation(y[:, 2 * i + k, :], bank[i % 8][:, k * T:(k + 1) * T], ACT.Copy, scale=cw[:, 2 * i + k, TAPS - 1:TAPS])
                        ins.then_inc(seq["tap0"], 1)
                    else:
                        if 2 * i == NCONV:
                            for s in range(2):
                                act.wait_ge(S["og_done"][s], before(b, NC))
                        act.activation(gate[:, 2 * i - NCONV:2 * i - NCONV + 2, :], bank[i % 8][:].rearrange("p (k t) -> p k t", k=2), ACT.Silu).then_inc(seq["gate_done"], 1)
                for i in range(NCONV // H):
                    act.wait_ge(seq["taps_done"], now(b, (i + 1) * H // 2, NCONV // 2))
                    act.activation(y[:, i * H:(i + 1) * H, :], y[:, i * H:(i + 1) * H, :], ACT.Silu).then_inc(seq["silu_done"], 1)
                act.wait_ge(seq["gate_done"], now(b, H // 2, H // 2))
                act.activation(gate[:], gate[:], ACT.Copy, scale=rmsw[:, 0:1]).then_inc(seq["gatew_done"], 1)
                act.wait_ge(seq["bg_psum"], now(b))
                act.activation(beta_t[:], bank[0][0:R, 0:NC * NK].rearrange("p (c i h) -> p c i h", c=NC, i=NH), ACT.Tanh, scale=0.5).then_inc(seq["tanh_done"], 1)
                act.wait_ge(seq["abs_done"], now(b))
                act.activation(ez[:], az[:], ACT.Exp, scale=-1.0).then_inc(seq["exp_z"], 1)
                act.wait_ge(seq["decay_psum"], now(b))
                for s in range(2):
                    act.wait_ge(S["kd_done"][s], before(b, NC))
                    act.wait_ge(S["ksg_done"][s], before(b, NC))
                    act.wait_ge(S["dec_done"][s], before(b, NC))
                act.activation(decays[:], bank[2][:, 0:3 * NC * H].rearrange("p (k c h) -> p k c h", k=3, c=NC), ACT.Exp).then_inc(seq["decay_done"], 1)
                act.preload_act_table_set("natural_log_exp_and_others")

                def copy_keys(s, n1, c1):
                    hs, tok = s * GH, act.snap(c1 * C)
                    act.wait_ge(S["ks_psum"][s], before(n1))
                    act.wait_ge(S["kt_psum"][s], before(n1))
                    act.sem_inc(carrier, 1)
                    for i in range(NH):
                        act.activation(kq[s][:, :, 0:R].rearrange("p h (t i) -> p h t i", i=NH)[:, :, :, i],
                                       y[:, NQ + i * H + hs:NQ + i * H + hs + GH, bass.ds(tok, C)], ACT.Copy)
                    act.activation(kq[s][:, :, R:P], y[:, hs:hs + GH, bass.ds(tok, C)], ACT.Copy).then_inc(S["kq_done"][s], 1)

                def squares(s, n1, parity, old):
                    act.wait_ge(S["kq_done"][s], now(n1))
                    act.wait_ge(S["rms_psum"][s], old)
                    act.activation(sq[parity][s][:], kq[s][:], ACT.Square).then_inc(S["sq_done"][s], 1)

                def copy_values(s, n1, c1):
                    tok = act.snap(c1 * C)
                    act.wait_ge(S["vt_psum"][s], before(n1))
                    act.sem_inc(carrier, 1)
                    for i in range(NH):
                        ins = act.activation(vt[s][:].rearrange("p h (t i) -> p h t i", i=NH)[:, :, :, i],
                                             y[:, NQ + NK + i * H + s * GH:NQ + NK + i * H + s * GH + GH, bass.ds(tok, C)], ACT.Copy)
                    ins.then_inc(S["v_done"][s], 1)

                def exponentials(s, n1):
                    act.wait_ge(S["at_done"][s], before(n1))
                    act.wait_ge(S["e_psum"][s], now(n1))
                    act.activation(ex[s][:], bk[s][1][0:R, :].rearrange("p (h j) -> p h j", j=P), ACT.Exp).then_inc(S["ex_done"][s], 1)

                def lengths(s, n1):
                    act.wait_ge(S["ss_psum"][s], now(n1))
                    act.activation(lnss[s][:], bk[s][1][0:R, 0:GH], ACT.Ln, bias=qeps[0:R, 0:1]).then_inc(S["ln_done"][s], 1)
                    act.wait_ge(S["ln_done"][s], now(n1))
                    act.wait_ge(S["vn_done"][s], before(n1))
                    act.activation(vlen[s][:], lnss[s][:], ACT.Exp, scale=0.5).then_inc(S["vlen_done"][s], 1)

                def prepare(step, n1, c1, parity, old):
                    if step == 0:
                        copy_keys(0, n1, c1)
                    if step == 1:
                        copy_keys(1, n1, c1)
                        for s in range(2):
                            squares(s, n1, parity, old)
                        for s in range(2):
                            exponentials(s, n1)
                    if step == 2:
                        for s in range(2):
                            copy_values(s, n1, c1)
                        for s in range(2):
                            lengths(s, n1)

                def norm_factor(n0):
                    for s in range(2):
                        act.wait_ge(S["rms_psum"][s], now(n0))
                        act.activation(lnf[s][:], bk[s][1][:, 0:P].rearrange("p (h j) -> p h j", j=C), ACT.Ln, bias=oeps[:, 0:1]).then_inc(S["lnf_done"][s], 1)
                    for s in range(2):
                        act.wait_ge(S["lnf_done"][s], now(n0))
                        act.activation(fac[s][:], lnf[s][:], ACT.Exp, scale=-0.5).then_inc(S["fac_done"][s], 1)

                def turn(n, c, parity, first, last):
                    for l in range(TRANSPOSES):
                        for s in range(2):
                            act.wait_ge(S["t_psum"][s], now(n, l + 1, TRANSPOSES))
                            act.activation(MT[s][:], bk[s][3][0:R, 0:GH * R].rearrange("p (h j) -> p h j", j=R), ACT.Copy).then_inc(S["t_done"][s], 1)
                        if l == 0 and not first:
                            norm_factor(n - 1)
                        if not last:
                            prepare(l, n + 1, c + 1, 1 - parity, before(n))
                    for s in range(2):
                        act.wait_ge(S["u_psum"][s], now(n))
                        act.activation(w[s][:], bk[s][1][0:R, :].rearrange("p (h j) -> p h j", j=DV), ACT.Copy).then_inc(S["w_done"][s], 1)
                    for s in range(2):
                        act.wait_ge(S["o_psum"][s], now(n))
                        act.wait_ge(S["otf_done"][s], before(n))
                        act.activation(ot[s][:], bk[s][3][:, 0:P].rearrange("p (h j) -> p h j", j=C), ACT.Copy).then_inc(S["o_done"][s], 1)
                        act.wait_ge(S["o_done"][s], now(n))
                        act.activation(osq[s][:], ot[s][:], ACT.Square).then_inc(S["osq_done"][s], 1)
                    if last:
                        norm_factor(n)

                for step in range(LEVELS + 1):
                    prepare(step, b * NC, 0, 0, before(b, NC))
                chunks(act, b, turn)

        @block.vector
        def _(dve):
            dve.wait_ge(weights_in, 128)
            dve.wait_ge(const_done, 1)
            NP2 = NCONV // 2
            with dve.Fori(0, NB) as b:
                dve.wait_ge(seq["xb_loaded"], now(b, 16, 16))
                dve.wait_ge(seq["bg_psum"], before(b))
                dve.tensor_copy(xb3[:], xb[:].unsqueeze(2).broadcast_to([P, T, NH])).then_inc(seq["xb3_done"], 1)
                for i in range(NP2):
                    dve.wait_ge(seq["tap0"], now(b, i + 1, NP2))
                    for shift in range(1, TAPS):
                        for k in range(2):
                            blk = 2 * i + k
                            if shift > 1:
                                dve.wait_ge(seq["tap_step"], now(b, i * 2 * (TAPS - 2) + (shift - 2) * 2 + k + 1, NP2 * 2 * (TAPS - 2)))
                            ins = dve.scalar_tensor_tensor(
                                out=y[:, blk, shift:T], in0=bank[i % 8][:, k * T:k * T + T - shift],
                                scalar=cw[:, blk, TAPS - 1 - shift:TAPS - shift], in1=y[:, blk, shift:T], op0=ALU.mult, op1=ALU.add)
                            if shift < TAPS - 1:
                                ins.then_inc(seq["tap_step"], 1)
                    ins.then_inc(seq["taps_done"], 1)
                dve.wait_ge(seq["tanh_done"], now(b))
                dve.tensor_scalar(beta_t[:], beta_t[:], 1.0, None, ALU.add).then_inc(seq["beta1_done"], 1)
                dve.wait_ge(seq["beta1_done"], now(b))
                dve.tensor_tensor(beta_s[:], beta_t[:], ranksel[:].unsqueeze(1).unsqueeze(3).broadcast_to([R, NC, NH, H]), ALU.mult).then_inc(seq["betas_done"], 1)
                dve.wait_ge(seq["betas_done"], now(b))
                dve.tensor_reduce(beta[:], beta_s[:].rearrange("p c i h -> p c h i"), AX.X, ALU.add).then_inc(seq["beta_done"], 1)
                dve.wait_ge(seq["bg_psum"], now(b))
                dve.tensor_tensor(z[:], bank[1][0:C, 0:NC * H].rearrange("p (c h) -> p c h", c=NC), dtb[:].unsqueeze(1).broadcast_to([C, NC, H]), ALU.add).then_inc(seq["z_done"], 1)
                dve.wait_ge(seq["z_done"], now(b))
                dve.tensor_scalar(zp[:], z[:], 0.0, None, ALU.max)
                dve.scalar_tensor_tensor(out=az[:], in0=z[:], scalar=-1.0, in1=z[:], op0=ALU.mult, op1=ALU.max).then_inc(seq["abs_done"], 1)
                dve.wait_ge(seq["exp_z"], now(b))
                dve.tensor_scalar(ez2[:], ez[:], 2.0, None, ALU.add).then_inc(seq["plus2"], 1)
                dve.wait_ge(seq["plus2"], now(b))
                dve.reciprocal(ezr[:], ez2[:]).then_inc(seq["recip_z"], 1)
                dve.wait_ge(seq["recip_z"], now(b))
                dve.tensor_tensor(sz[:], ez[:], ezr[:], ALU.mult).then_inc(seq["s_done"], 1)
                dve.wait_ge(seq["s_done"], now(b))
                dve.tensor_tensor(sz2[:], sz[:], sz[:], ALU.mult).then_inc(seq["s2_done"], 1)
                dve.wait_ge(seq["s2_done"], now(b))
                NS = len(ATANH) - 1
                dve.tensor_scalar(poly[:], sz2[:], ATANH[NS], ATANH[NS - 1], ALU.mult, ALU.add).then_inc(seq["horner"], 1)
                steps = 1
                for j in range(NS - 2, -1, -1):
                    dve.wait_ge(seq["horner"], now(b, steps, 2 * NS - 1))
                    dve.tensor_tensor(poly[:], poly[:], sz2[:], ALU.mult).then_inc(seq["horner"], 1)
                    dve.wait_ge(seq["horner"], now(b, steps + 1, 2 * NS - 1))
                    dve.tensor_scalar(poly[:], poly[:], ATANH[j], None, ALU.add).then_inc(seq["horner"], 1)
                    steps += 2
                dve.wait_ge(seq["horner"], now(b, 2 * NS - 1, 2 * NS - 1))
                dve.tensor_tensor(poly[:], poly[:], sz[:], ALU.mult).then_inc(seq["softplus"], 1)
                dve.wait_ge(seq["softplus"], now(b, 1, 2))
                dve.scalar_tensor_tensor(out=poly[:], in0=poly[:], scalar=2.0, in1=zp[:], op0=ALU.mult, op1=ALU.add).then_inc(seq["softplus"], 1)
                dve.wait_ge(seq["softplus"], now(b, 2, 2))
                dve.wait_ge(expa_done, 1)
                dve.tensor_tensor(poly[:], poly[:], expa[:].unsqueeze(1).broadcast_to([C, NC, H]), ALU.mult).then_inc(seq["decay_in"], 1)
                dve.wait_ge(seq["decay_in"], now(b))
                for s in range(2):
                    dve.wait_ge(S["gr_done"][s], before(b, NC))
                dve.tensor_scalar(g[:], poly[:], -1.0, -BIG, ALU.mult, ALU.max).then_inc(seq["g_done"], 1)

                def decayed_products(s, n1, parity, old):
                    dve.wait_ge(S["gram"][s], now(n1))
                    dve.wait_ge(S["ex_done"][s], now(n1))
                    dve.wait_ge(S["o_psum"][s], old)
                    dve.tensor_tensor(at[parity][s][:], bk[s][0][0:R, :].rearrange("p (h j) -> p h j", j=P), ex[s][:], ALU.mult).then_inc(S["at_done"][s], 1)

                def diagonal(s, n1, c1):
                    dve.wait_ge(S["ln_done"][s], now(n1))
                    dve.tensor_scalar(sse[s][:], bk[s][1][0:R, 0:GH], QEPS, None, ALU.add).then_inc(S["sse_done"][s], 1)
                    dve.wait_ge(S["sse_done"][s], now(n1))
                    dve.reciprocal(inv[s][:], sse[s][:]).then_inc(S["inv_done"][s], 1)
                    dve.wait_ge(S["inv_done"][s], now(n1))
                    dve.wait_ge(S["m0_done"][s], before(n1))
                    dve.tensor_tensor(bp[s][:].unsqueeze(2), inv[s][:].unsqueeze(2), per_head(beta, c1, s), ALU.mult).then_inc(S["bp_done"][s], 1)
                    dve.wait_ge(S["bp_done"][s], now(n1))
                    dve.tensor_tensor(x_first[s][:], bp[s][:].unsqueeze(2).broadcast_to([R, GH, NH]),
                                      ranksel[:].unsqueeze(1).broadcast_to([R, GH, NH]), ALU.mult).then_inc(S["x_step"][s], 1)

                def token_blocks(s, k, n1):
                    dve.wait_ge(S["ax_psum"][s], now(n1, k + 1, 2))
                    dve.tensor_tensor(bax[s][:], bk[s][0][0:R, 0:GH * NH].rearrange("p (h i) -> p h i", i=NH),
                                      bp[s][:].unsqueeze(2).broadcast_to([R, GH, NH]), ALU.mult).then_inc(S["x_step"][s], 1)
                    dve.wait_ge(S["x_step"][s], now(n1, 2 * k + 2, XSTEPS))
                    dve.tensor_tensor(x_next[s][:], x_first[s][:], bax[s][:], ALU.subtract).then_inc(S["x_step"][s], 1)

                def natural_keys(s, n1, c1, parity, old):
                    dve.wait_ge(S["kt_psum"][s], now(n1))
                    dve.wait_ge(S["su_psum"][s], old)
                    dve.tensor_tensor(kd[parity][s][:], bk[s][0][0:R, :].rearrange("p (h j) -> p h j", j=P),
                                      per_head(decays[0:R, 1], c1, s).broadcast_to([R, GH, P]), ALU.mult).then_inc(S["kd_done"][s], 1)

                def natural_values(s, n1):
                    dve.wait_ge(S["vt_psum"][s], now(n1))
                    dve.wait_ge(S["vlen_done"][s], now(n1))
                    dve.wait_ge(S["rhs_done"][s], before(n1))
                    dve.tensor_tensor(vn[s][:], bk[s][1][0:R, :].rearrange("p (h j) -> p h j", j=DV),
                                      vlen[s][:].unsqueeze(2).broadcast_to([R, GH, DV]), ALU.mult).then_inc(S["vn_done"][s], 1)

                def prepare(step, n1, c1, parity, old):
                    if step == 1:
                        for s in range(2):
                            decayed_products(s, n1, parity, old)
                    if step == 2:
                        for s in range(2):
                            diagonal(s, n1, c1)
                        natural_keys(0, n1, c1, parity, old)
                        natural_keys(1, n1, c1, parity, old)
                    if step == 3:
                        for s in range(2):
                            natural_values(s, n1)
                    if step == 4:
                        token_blocks(0, 0, n1)
                        token_blocks(1, 0, n1)
                    if step == 5:
                        token_blocks(0, 1, n1)
                        token_blocks(1, 1, n1)

                def turn(n, c, parity, first, last):
                    for l in range(LEVELS):
                        for s in range(2):
                            dve.wait_ge(S["p_psum"][s], now(n, l + 1, LEVELS))
                            mask = block_mask[:, l, :].unsqueeze(1).broadcast_to([R, GH, HALF])
                            dve.tensor_tensor(fh(pl[s][:], l), fh(bk[s][2][0:R, 0:GH * R].rearrange("p (h j) -> p h j", h=GH), l), compact(mask, l), ALU.mult).then_inc(S["p_done"][s], 1)
                        for s in range(2):
                            dve.wait_ge(S["m_psum"][s], now(n, l + 1, LEVELS))
                            if l == 0:
                                dve.wait_ge(S["m0_done"][s], now(n))
                            else:
                                dve.wait_ge(S["m_done"][s], now(n, l, LEVELS))
                            new = bk[s][2][0:R, 0:GH * R].rearrange("p (h j) -> p h j", h=GH)
                            dve.tensor_tensor(fh(M[s][:], l), fh(M[s][:], l), fh(new, l), ALU.add).then_inc(S["m_done"][s], 1)
                        if l == 0:
                            for s in range(2):
                                dve.wait_ge(S["ks_psum"][s], now(n))
                                dve.wait_ge(S["o_psum"][s], before(n))
                                dve.tensor_tensor(ksg[s][:], bk[s][0][:].rearrange("p (h j) -> p h j", j=DV),
                                                  per_head(decays[:, 0], c, s).broadcast_to([P, GH, DV]), ALU.mult).then_inc(S["ksg_done"][s], 1)
                        if not last:
                            prepare(l, n + 1, c + 1, 1 - parity, before(n))
                    if not last:
                        prepare(LEVELS, n + 1, c + 1, 1 - parity, before(n))
                    for s in range(2):
                        dve.wait_ge(S["su_psum"][s], now(n))
                        dve.wait_ge(S["dec_done"][s], now(n))
                        dve.tensor_tensor(st[s][:], st_dec[s][:], bk[s][0][:].rearrange("p (h j) -> p h j", j=DV), ALU.add).then_inc(S["st_done"][s], 1)

                for step in range(LEVELS + 1):
                    prepare(step, b * NC, 0, 0, before(b, NC))
                chunks(dve, b, turn)
                dve.wait_ge(seq["wo_psum"], now(b))
                dve.wait_ge(seq["x1_loaded"], now(b, 16, 16))
                dve.wait_ge(seq["x2_stored"], before(b, 16))
                dve.tensor_tensor(x2[:], x1[:], bank[0][:, 0:TT * D].rearrange("p (t d) -> p t d", d=D), ALU.add).then_inc(seq["x2_done"], 1)

        @block.tensor
        def _(pe):
            pe.wait_ge(weights_in, 128)
            pe.wait_ge(const_done, 1)
            NPB = (NCONV + H) // 2
            with pe.Fori(0, NB) as b:
                pe.wait_ge(seq["xb_loaded"], now(b, 16, 16))
                pe.wait_ge(seq["x2_done"], before(b))
                for s in range(2):
                    pe.wait_ge(S["st_done"][s], before(b, NC))
                    pe.wait_ge(S["fac_done"][s], before(b, NC))
                    pe.wait_ge(S["o_done"][s], before(b, NC))
                for i in range(NPB):
                    if 8 <= i:
                        j = i - 8
                        pe.wait_ge(seq["taps_done"], now(b, j + 1, NCONV // 2))
                    for k in range(2):
                        blk = 2 * i + k
                        ins = pe.matmul(bank[i % 8][:, k * T:(k + 1) * T], wp[:, blk * P:(blk + 1) * P], xb[:], start=True, stop=True)
                    ins.then_inc(seq["proj"], 1)
                pe.wait_ge(seq["taps_done"], now(b, NCONV // 2, NCONV // 2))
                pe.wait_ge(seq["gate_done"], now(b, H // 2, H // 2))
                pe.wait_ge(seq["xb3_done"], now(b))
                for c in range(NC):
                    pe.matmul(bank[0][0:R, c * NK:(c + 1) * NK], xb3[:, c * C:(c + 1) * C, :].rearrange("p t i -> p (t i)"), wb[:], start=True, stop=True)
                for c in range(NC):
                    ins = pe.matmul(bank[1][0:C, c * H:(c + 1) * H], xb[:, c * C:(c + 1) * C], wa[:], start=True, stop=True)
                ins.then_inc(seq["bg_psum"], 1)
                pe.wait_ge(seq["g_done"], now(b))
                gv = g[:].rearrange("p c h -> p (c h)")
                for k, lhs in enumerate((upto, later_only, ones)):
                    ins = pe.matmul(bank[2][:, k * NC * H:(k + 1) * NC * H], lhs[0:C, :], gv, start=True, stop=True)
                ins.then_inc(seq["decay_psum"], 1)
                pe.wait_ge(seq["silu_done"], now(b, NCONV // H, NCONV // H))
                pe.wait_ge(seq["decay_done"], now(b))
                pe.wait_ge(seq["tanh_done"], now(b))
                pe.sem_inc(carrier, 1)

                def exponent(s, n1, old):
                    pe.wait_ge(S["gr_done"][s], now(n1))
                    pe.wait_ge(S["w_done"][s], before(n1) if old is None else old)
                    pe.wait_ge(S["lnf_done"][s], before(n1) if old is None else old)
                    pe.matmul(bk[s][1][0:R, :], later[:], gr[s][:].rearrange("p h j -> p (h j)"), start=True, stop=True).then_inc(S["e_psum"][s], 1)

                def gram(s, n1):
                    pe.wait_ge(S["kq_done"][s], now(n1))
                    pe.wait_ge(S["ksg_done"][s], before(n1))
                    for h in range(GH):
                        ins = pe.matmul(bk[s][0][0:R, h * P:(h + 1) * P], kq[s][:, h, 0:R], kq[s][:, h, :], start=True, stop=True)
                    ins.then_inc(S["gram"][s], 1)

                def square_sums(s, n1, parity):
                    pe.wait_ge(S["sq_done"][s], now(n1))
                    pe.wait_ge(S["ex_done"][s], now(n1))
                    for h in range(GH):
                        ins = pe.matmul(bk[s][1][0:R, h:h + 1], sq[parity][s][:, h, 0:R], ones[:, 0:1], start=True, stop=True)
                    ins.then_inc(S["ss_psum"][s], 1)

                def transpose_keys(s, n1):
                    pe.wait_ge(S["at_done"][s], now(n1))
                    for h in range(GH):
                        ins = pe.transpose(bk[s][0][0:R, h * P:(h + 1) * P], kq[s][:, h, 0:R], ident[:])
                    ins.then_inc(S["kt_psum"][s], 1)

                def transpose_values(s, n1):
                    pe.wait_ge(S["ln_done"][s], now(n1))
                    pe.wait_ge(S["sse_done"][s], now(n1))
                    pe.wait_ge(S["v_done"][s], now(n1))
                    for h in range(GH):
                        ins = pe.transpose(bk[s][1][0:R, h * P:(h + 1) * P], vt[s][:, h, :], ident[:])
                    ins.then_inc(S["vt_psum"][s], 1)

                def own_times_x(s, k, n1):
                    if k == 0:
                        pe.wait_ge(S["own_done"][s], now(n1))
                        pe.wait_ge(S["kd_done"][s], now(n1))
                    pe.wait_ge(S["x_step"][s], now(n1, 2 * k + 1, XSTEPS))
                    x = x_first_full if k == 0 else x_next_full
                    for h in range(GH):
                        ins = pe.matmul(bk[s][0][0:R, h * NH:(h + 1) * NH], own_full[s][:, h, :], x[s][:, h, :], start=True, stop=True)
                    ins.then_inc(S["ax_psum"][s], 1)

                def prepare(step, n1, parity, old):
                    if step == 0:
                        exponent(0, n1, old)
                        exponent(1, n1, old)
                        gram(0, n1)
                    if step == 1:
                        gram(1, n1)
                        square_sums(0, n1, parity)
                        square_sums(1, n1, parity)
                        transpose_keys(0, n1)
                    if step == 2:
                        transpose_keys(1, n1)
                        transpose_values(0, n1)
                        transpose_values(1, n1)
                    if step == 3:
                        own_times_x(0, 0, n1)
                        own_times_x(1, 0, n1)
                    if step == 4:
                        own_times_x(0, 1, n1)
                    if step == 5:
                        own_times_x(1, 1, n1)

                def mean_squares(n0, parity):
                    for s in range(2):
                        pe.wait_ge(S["osq_done"][s], now(n0))
                        pe.matmul(bk[s][1][:, 0:P], mean_dv[:], osq[s][:].rearrange("p h j -> p (h j)"), start=True, stop=False)
                        pe.matmul(bk[s][1][:, 0:P].rearrange("p (h j) -> p h j", h=GH), mean_eps[:], sq[parity][s][:, :, R:P], start=False, stop=True).then_inc(S["rms_psum"][s], 1)

                def transpose_m(s):
                    for h in range(GH):
                        ins = pe.transpose(bk[s][3][0:R, h * R:(h + 1) * R], M[s][:, h, :], ident[0:R, 0:R])
                    ins.then_inc(S["t_psum"][s], 1)

                def turn(n, c, parity, first, last):
                    for s in range(2):
                        pe.wait_ge(S["m0_done"][s], now(n))
                        pe.wait_ge(S["o_done"][s], before(n))
                        transpose_m(s)
                    for l in range(LEVELS):
                        for s in range(2):
                            if l == 0:
                                pe.wait_ge(S["m0_done"][s], now(n))
                            else:
                                pe.wait_ge(S["m_done"][s], now(n, l, LEVELS))
                            for h in range(GH):
                                ins = pe.matmul(bk[s][2][0:R, h * R:(h + 1) * R], at_full[parity][s][:, h, 0:R], M_full[s][:, h, :], start=True, stop=True)
                            ins.then_inc(S["p_psum"][s], 1)
                        for s in range(2):
                            pe.wait_ge(S["p_done"][s], now(n, l + 1, LEVELS))
                            pe.wait_ge(S["t_done"][s], now(n, l + 1, TRANSPOSES))
                            for h in range(GH):
                                ins = pe.matmul(bk[s][2][0:R, h * R:(h + 1) * R], MT_full[s][:, h, :], pl_full[s][:, h, :], start=True, stop=True)
                            ins.then_inc(S["m_psum"][s], 1)
                        if l == 0:
                            for s in range(2):
                                pe.wait_ge(S["st_done"][s], before(n))
                                pe.wait_ge(S["kd_done"][s], now(n))
                                for h in range(GH):
                                    ins = pe.matmul(bk[s][0][:, h * P:(h + 1) * P], kq[s][:, h, :], st[s][:, h, :], start=True, stop=True)
                                ins.then_inc(S["ks_psum"][s], 1)
                        for s in range(2):
                            pe.wait_ge(S["m_done"][s], now(n, l + 1, LEVELS))
                            transpose_m(s)
                        if l == 0 and not first:
                            mean_squares(n - 1, 1 - parity)
                        if not last:
                            prepare(l, n + 1, 1 - parity, before(n))
                    for s in range(2):
                        pe.wait_ge(S["rhs_done"][s], now(n))
                        pe.wait_ge(S["vn_done"][s], now(n) if last else now(n + 1))
                        pe.wait_ge(S["t_done"][s], now(n, TRANSPOSES, TRANSPOSES))
                        if last:
                            pe.wait_ge(S["lnf_done"][s], before(n))
                        for h in range(GH):
                            ins = pe.matmul(bk[s][1][0:R, h * P:(h + 1) * P], MT_full[s][:, h, :], rhs_full[s][:, h, :], start=True, stop=True)
                        ins.then_inc(S["u_psum"][s], 1)
                        if s == 0 and not last:
                            prepare(LEVELS, n + 1, 1 - parity, before(n))
                    for s in range(2):
                        pe.wait_ge(S["w_done"][s], now(n))
                        pe.wait_ge(S["ksg_done"][s], now(n))
                        pe.wait_ge(S["x_step"][s], now(n if last else n + 1, XSTEPS, XSTEPS))
                        for h in range(GH):
                            ins = pe.matmul(bk[s][0][:, h * P:(h + 1) * P], kd_full[parity][s][:, h, :], w_full[s][:, h, :], start=True, stop=True)
                        ins.then_inc(S["su_psum"][s], 1)
                        for h in range(GH):
                            out = bk[s][3][:, h * C:(h + 1) * C]
                            pe.matmul(out, w_full[s][:, h, :], at_full[parity][s][:, h, R:P], start=True, stop=False)
                            ins = pe.matmul(out, ksg[s][:, h, :], ident[:, R:P], start=False, stop=True)
                        ins.then_inc(S["o_psum"][s], 1)
                    if last:
                        mean_squares(n, parity)

                for step in range(LEVELS + 1):
                    prepare(step, b * NC, 0, None)
                pe.wait_ge(seq["st_zero"], now(b, 2, 2))
                pe.sem_inc(carrier, 1)
                chunks(pe, b, turn)
                for s in range(2):
                    pe.wait_ge(S["og_done"][s], now(b, NC, NC))
                    pe.wait_ge(S["st_done"][s], now(b, NC, NC))
                for t in range(TT):
                    for h in range(H):
                        ins = pe.matmul(bank[0][:, t * D:(t + 1) * D], og[:, h, t * P:(t + 1) * P], wo[:, h, :], start=h == 0, stop=h == H - 1)
                ins.then_inc(seq["wo_psum"], 1)
    end_phase(nc, m)


def expert_layer(nc, x2_dram, xn2t_dram, router_t, w1_t, b1_t, w2_t, b2, out):
    E, F, TB = 8, 512, 512
    FB, NT = F // P, TB // P
    LOOPS = NTOK // TB
    with ExitStack() as ctx:
        m = Memory(nc, ctx, "moe")
        rw = m.sb("rw", [P, E])
        w1 = m.sb("w1", [P, E, F])
        b1 = m.sb("b1", [P, E, FB])
        w2 = m.sb("w2", [P, E, FB, D])
        b2s = m.sb("b2s", [E, D])
        ident = m.sb("ident", [P, P])
        expert_id = m.sb("expert_id", [P, E])
        xs = m.sb("xs", [P, 2, TB])
        x2 = m.sb("x2", [P, NT, D])
        top = m.sb("top", [P, NT, 8])
        topi = m.sb("topi", [P, NT, 8], u32)
        topf = m.sb("topf", [P, NT, 2])
        gap = m.sb("gap", [P, NT])
        egap = m.sb("egap", [P, NT])
        den = m.sb("den", [P, NT])
        wt = m.sb("wt", [P, 2, NT])
        first = m.sb("first", [P, NT, E])
        second = m.sb("second", [P, NT, E])
        gates = m.sb("gates", [P, NT, E])
        gatesT = m.sb("gatesT", [E, NT, P])
        h1 = m.sb("h1", [P, 2, FB, TB])
        acc = m.sb("acc", [P, NT, D])
        bank = m.banks(8)

        weights_in = m.sem("weights_in")
        const_step = m.sem("const_step")
        const_done = m.sem("const_done")
        UNPRIMED = len(m.semaphores)
        (x_loaded, x2_loaded, logits, top_done, topi_done, topf_done, gap_done, egap_done, den_done, wt0_done, wt_done,
         first_done, second_done, gates_done, gatesT_psum, gatesT_done, bias_psum, hidden, h1_done, expert_out, acc_done,
         stored) = [m.sem(k) for k in (
             "x_loaded x2_loaded logits top_done topi_done topf_done gap_done egap_done den_done wt0_done wt_done "
             "first_done second_done gates_done gatesT_psum gatesT_done bias_psum hidden h1_done expert_out acc_done stored").split()]
        carrier = m.sem("carrier")
        block = ctx.enter_context(nc.Block())

        @block.sync
        def _(sp):
            for s in m.semaphores[UNPRIMED:]:
                sp.sem_inc(s, 1)
            for dst, src in ((rw[:], router_t), (w1[:], w1_t), (b1[:], b1_t), (b2s[:], b2), (w2[:], w2_t)):
                sp.dma_start(dst, src).then_inc(weights_in, 16)
            with sp.Fori(0, LOOPS) as n:
                tok = sp.snap(n * TB)
                sp.wait_ge(hidden, before(n, E * FB))
                sp.sem_inc(carrier, 1)
                sp.dma_start(xs[:, 0, :], xn2t_dram[:, bass.ds(tok, TB)]).then_inc(x_loaded, 16)
                sp.wait_ge(acc_done, before(n, NT * (E + 1)))
                sp.sem_inc(carrier, 1)
                sp.dma_start(x2[:], x2_dram[bass.ds(tok, TB), :].rearrange("(t p) d -> p t d", p=P)).then_inc(x2_loaded, 16)
                sp.wait_ge(acc_done, now(n, NT * (E + 1), NT * (E + 1)))
                sp.sem_inc(carrier, 1)
                sp.dma_start(out[bass.ds(tok, TB), :].rearrange("(t p) d -> p t d", p=P), acc[:]).then_inc(stored, 16)
            sp.wait_ge(stored, 16 * LOOPS + 1)

        @block.gpsimd
        def _(pool):
            pool.memset(ident[:], 0.0).then_inc(const_step, 1)
            pool.wait_ge(const_step, 1)
            pool.affine_select(out=ident[:], in_=ident[:], compare_op=ALU.not_equal, fill=1.0, base=0,
                               pattern=[[-1, P]], channel_multiplier=1).then_inc(const_done, 1)
            for e in range(E):
                ins = pool.memset(expert_id[:, e:e + 1], float(e))
            ins.then_inc(const_done, 1)

        @block.scalar
        def _(act):
            act.wait_ge(weights_in, 80)
            with act.Fori(0, LOOPS) as n:
                act.wait_ge(gap_done, now(n))
                act.activation(egap[:], gap[:], ACT.Exp).then_inc(egap_done, 1)
                act.wait_ge(gatesT_psum, now(n))
                act.activation(gatesT[:], bank[7][0:E, :].rearrange("p (t q) -> p t q", q=P), ACT.Copy).then_inc(gatesT_done, 1)
                for e in range(E):
                    if e >= 2:
                        act.wait_ge(expert_out, now(n, e - 1, E))
                    else:
                        act.wait_ge(expert_out, before(n, E))
                    for f in range(FB):
                        act.wait_ge(hidden, now(n, e * FB + f + 1, E * FB))
                        act.activation(h1[:, e % 2, f, :], bank[f][:], ACT.Gelu, bias=b1[:, e, f:f + 1]).then_inc(h1_done, 1)

        @block.vector
        def _(dve):
            dve.wait_ge(const_done, 2)
            with dve.Fori(0, LOOPS) as n:
                dve.wait_ge(logits, now(n))
                dve.sem_inc(carrier, 1)
                for t in range(NT):
                    dve.max(top[:, t, :], bank[6][:, t * E:(t + 1) * E]).then_inc(top_done, 1)
                dve.wait_ge(top_done, now(n, NT, NT))
                dve.sem_inc(carrier, 1)
                for t in range(NT):
                    dve.max_index(topi[:, t, :], top[:, t, :], bank[6][:, t * E:(t + 1) * E]).then_inc(topi_done, 1)
                dve.tensor_tensor(gap[:], top[:, :, 1], top[:, :, 0], ALU.subtract).then_inc(gap_done, 1)
                dve.wait_ge(topi_done, now(n, NT, NT))
                dve.tensor_copy(topf[:], topi[:, :, 0:2]).then_inc(topf_done, 1)
                dve.wait_ge(egap_done, now(n))
                dve.tensor_scalar(den[:], egap[:], 1.0, None, ALU.add).then_inc(den_done, 1)
                dve.wait_ge(den_done, now(n))
                dve.reciprocal(wt[:, 0, :], den[:]).then_inc(wt0_done, 1)
                dve.wait_ge(wt0_done, now(n))
                dve.tensor_tensor(wt[:, 1, :], wt[:, 0, :], egap[:], ALU.mult).then_inc(wt_done, 1)
                dve.wait_ge(wt_done, now(n))
                dve.wait_ge(topf_done, now(n))
                for t in range(NT):
                    dve.tensor_scalar(first[:, t, :], expert_id[:], topf[:, t, 0:1], wt[:, 0, t:t + 1], ALU.is_equal, ALU.mult).then_inc(first_done, 1)
                    dve.tensor_scalar(second[:, t, :], expert_id[:], topf[:, t, 1:2], wt[:, 1, t:t + 1], ALU.is_equal, ALU.mult).then_inc(second_done, 1)
                dve.wait_ge(first_done, now(n, NT, NT))
                dve.wait_ge(second_done, now(n, NT, NT))
                dve.tensor_tensor(gates[:], first[:], second[:], ALU.add).then_inc(gates_done, 1)
                dve.wait_ge(bias_psum, now(n))
                dve.wait_ge(x2_loaded, now(n, 16, 16))
                dve.wait_ge(stored, before(n, 16))
                for t in range(NT):
                    dve.tensor_tensor(acc[:, t, :], x2[:, t, :], bank[7][:, t * P:(t + 1) * P], ALU.add).then_inc(acc_done, 1)
                for e in range(E):
                    dve.wait_ge(expert_out, now(n, e + 1, E))
                    for t in range(NT):
                        dve.wait_ge(acc_done, now(n, e * NT + t + 1, NT * (E + 1)))
                        dve.scalar_tensor_tensor(out=acc[:, t, :], in0=bank[4 + e % 2][:, t * D:(t + 1) * D], scalar=gates[:, t, e:e + 1],
                                                 in1=acc[:, t, :], op0=ALU.mult, op1=ALU.add).then_inc(acc_done, 1)

        @block.tensor
        def _(pe):
            pe.wait_ge(weights_in, 80)
            pe.wait_ge(const_done, 2)
            with pe.Fori(0, LOOPS) as n:
                pe.wait_ge(x_loaded, now(n, 16, 16))
                pe.wait_ge(topi_done, before(n, NT))
                for t in range(NT):
                    ins = pe.matmul(bank[6][:, t * E:(t + 1) * E], xs[:, 0, t * P:(t + 1) * P], rw[:], start=True, stop=True)
                ins.then_inc(logits, 1)

                def hidden_layer(e):
                    for f in range(FB):
                        if e == 0:
                            pe.wait_ge(h1_done, before(n, E * FB))
                        else:
                            pe.wait_ge(h1_done, now(n, (e - 1) * FB + f + 1, E * FB))
                        pe.matmul(bank[f][:], w1[:, e, f * P:(f + 1) * P], xs[:, 0, :], start=True, stop=True).then_inc(hidden, 1)

                def output_layer(e):
                    pe.wait_ge(h1_done, now(n, (e + 1) * FB, E * FB))
                    if e >= 2:
                        pe.wait_ge(acc_done, now(n, e * NT, NT * (E + 1)))
                    else:
                        pe.wait_ge(acc_done, before(n, NT * (E + 1)))
                    for t in range(NT):
                        for f in range(FB):
                            ins = pe.matmul(bank[4 + e % 2][:, t * D:(t + 1) * D], h1[:, e % 2, f, t * P:(t + 1) * P], w2[:, e, f, :],
                                            start=f == 0, stop=f == FB - 1)
                    ins.then_inc(expert_out, 1)

                hidden_layer(0)
                pe.wait_ge(gates_done, now(n))
                pe.wait_ge(acc_done, before(n, NT * (E + 1)))
                for t in range(NT):
                    ins = pe.transpose(bank[7][0:E, t * P:(t + 1) * P], gates[:, t, :], ident[:])
                ins.then_inc(gatesT_psum, 1)
                pe.wait_ge(gatesT_done, now(n))
                for t in range(NT):
                    ins = pe.matmul(bank[7][:, t * D:(t + 1) * D], gatesT[:, t, :], b2s[:], start=True, stop=True)
                ins.then_inc(bias_psum, 1)
                for e in range(E):
                    if e + 1 < E:
                        hidden_layer(e + 1)
                    output_layer(e)
    end_phase(nc, m)


def forward(nc, *, x, w_qkv, w_out, w_fp8_t, ffn_bias, in_scale, w_scale, w_proj, conv_w, w_beta, w_decay,
            a_log, dt_bias, rms_w, w_o, router_t, w1_t, b1_t, w2_t, b2, out):
    x1 = nc.dram_tensor("x1_dram", (NTOK, D), fp32, kind="Internal").ap()
    x2 = nc.dram_tensor("x2_dram", (NTOK, D), fp32, kind="Internal").ap()
    xn2t = nc.dram_tensor("xn2t_dram", (D, NTOK), fp32, kind="Internal").ap()
    local_attention_layer(nc, x, w_qkv, w_out, w_fp8_t, ffn_bias, in_scale, w_scale, x1, xn2t)
    delta_attention_layer(nc, x1, xn2t, w_proj, conv_w, w_beta, w_decay, a_log, dt_bias, rms_w, w_o, x2)
    expert_layer(nc, x2, xn2t, router_t, w1_t, b1_t, w2_t, b2, out)


def kernel(**inputs):
    import numpy as _np
    import concourse.bacc as _bacc
    from concourse.bass_utils import run_bass_kernel_spmd as _run

    I = {k: _np.asarray(v) for k, v in inputs.items()}
    H, E = 8, 8
    channels = lambda a, n: a.reshape(n, P, -1).transpose(1, 0, 2)
    laid = {
        "x": I["L0_attn_x"].reshape(NTOK, D),
        "w_qkv": I["L0_attn_w_qkv"],
        "w_out": I["L0_attn_w_out"],
        "w_fp8_t": I["L0_ffn_weight_fp8"].T,
        "ffn_bias": I["L0_ffn_bias"].reshape(1, D),
        "in_scale": I["L0_ffn_input_scale"].reshape(1, 1),
        "w_scale": I["L0_ffn_weight_scale"].reshape(1, 1),
        "w_proj": _np.concatenate([I["L1_attn_" + k] for k in ("Wq", "Wk", "Wv", "Wg")], 1),
        "conv_w": channels(_np.concatenate([I["L1_attn_conv_" + k] for k in "qkv"], 0), 7 * H),
        "w_beta": I["L1_attn_Wb"],
        "w_decay": I["L1_attn_Wa"],
        "a_log": I["L1_attn_A_log"].reshape(1, H),
        "dt_bias": I["L1_attn_dt_bias"].reshape(1, H),
        "rms_w": I["L1_attn_rms_weight"].reshape(P, 1),
        "w_o": channels(I["L1_attn_Wo"], H),
        "router_t": I["L1_ffn_router_w"].T,
        "w1_t": I["L1_ffn_w1"].transpose(2, 0, 1),
        "b1_t": I["L1_ffn_b1"].reshape(E, -1, P).transpose(2, 0, 1),
        "w2_t": I["L1_ffn_w2"].reshape(E, D, -1, P).transpose(3, 0, 2, 1),
        "b2": I["L1_ffn_b2"],
    }
    nc = _bacc.Bacc("TRN2", target_bir_lowering=False, num_devices=1)
    arrays, args = {}, {}
    for name, a in laid.items():
        a = _np.ascontiguousarray(a)
        arrays[f"in_{name}"] = a
        args[name] = nc.dram_tensor(f"in_{name}", a.shape, mybir.dt.from_np(a.dtype), kind="ExternalInput").ap()
    args["out"] = nc.dram_tensor("out_0", (NTOK, D), fp32, kind="ExternalOutput").ap()
    forward(nc, **args)
    r = _run(nc, [arrays], core_ids=[0])
    return r.results[0]["out_0"].reshape(NB, T, D)
```
